# Optimizing a Trainium2 kernel written in Bass

```python
import numpy as np
import jax
import jax.numpy as jnp

def _softmax(x, axis=-1):
    return jax.nn.softmax(x, axis=axis)

def _gelu(x):
    return jax.nn.gelu(x, approximate=True)

def _silu(x):
    return jax.nn.silu(x)

def _sigmoid(x):
    return jax.nn.sigmoid(x)

def _layernorm(x, axis=-1, eps=1e-05):
    m = jnp.mean(x, axis=axis, keepdims=True)
    v = jnp.var(x, axis=axis, keepdims=True)
    return (x - m) / jnp.sqrt(v + eps)

def _scatter_add(tgt, idx, src, axis=0):
    return tgt.at[idx].add(src)

def _segment_sum(src, seg, n):
    return jax.ops.segment_sum(src, seg, n)
kernel_name = 'mk_rec_standalone_d1_rec_r8_a3606c'

def setup_inputs(seed: int=0):
    np.random.seed(seed)
    _w = jnp.asarray

    def _rec_inputs():
        import jax
        import jax.numpy as jnp
        _rk = jax.random.key(seed)
        r_queries = -0.00154741 + 1.00114 * jax.random.normal(jax.random.fold_in(_rk, 1), (2048, 128), jnp.float32)
        r_user_behaviors = -0.00010897 + 0.999902 * jax.random.normal(jax.random.fold_in(_rk, 2), (2048, 200, 128), jnp.float32)
        r_masks = jax.random.randint(jax.random.fold_in(_rk, 3), (2048, 200), 0, 2, jnp.int32)
        return (r_queries, r_user_behaviors, r_masks)
    r_queries, r_user_behaviors, r_masks = _rec_inputs()

    def _L0_rec_setup():
        import jax, jax.numpy as jnp
        import numpy as np
        NEG_LARGE = -2.0 ** 32 + 1.0
        key = jax.random.key(seed)
        ks = jax.random.split(key, 8)
        B, L, D = (256, 200, 64)
        H1, H2 = (80, 40)
        queries = jax.random.normal(ks[0], (B, 2 * D), dtype=jnp.float32)
        user_behaviors = jax.random.normal(ks[1], (B, L, 2 * D), dtype=jnp.float32)
        masks = jax.random.randint(ks[2], (B, L), 0, 2, dtype=jnp.int32)
        s = 1.0 / np.sqrt(8 * D)
        w1 = jax.random.uniform(ks[3], (8 * D, H1), minval=-s, maxval=s, dtype=jnp.float32)
        b1 = jnp.zeros((H1,), jnp.float32)
        s2 = 1.0 / np.sqrt(H1)
        w2 = jax.random.uniform(ks[4], (H1, H2), minval=-s2, maxval=s2, dtype=jnp.float32)
        b2 = jnp.zeros((H2,), jnp.float32)
        s3 = 1.0 / np.sqrt(H2)
        w3 = jax.random.uniform(ks[5], (H2, 1), minval=-s3, maxval=s3, dtype=jnp.float32)
        b3 = jnp.zeros((1,), jnp.float32)
        return {'queries': queries, 'user_behaviors': user_behaviors, 'masks': masks, 'w1': w1, 'b1': b1, 'w2': w2, 'b2': b2, 'w3': w3, 'b3': b3}
    _L0_rec_all = _L0_rec_setup()
    _L0_rec_in = {k: v for k, v in _L0_rec_all.items() if k in ('w1', 'b1', 'w2', 'b2', 'w3', 'b3')}
    del _L0_rec_all
    return {'r_queries': r_queries, 'r_user_behaviors': r_user_behaviors, 'r_masks': r_masks, 'L0_rec_w1': _L0_rec_in['w1'], 'L0_rec_b1': _L0_rec_in['b1'], 'L0_rec_w2': _L0_rec_in['w2'], 'L0_rec_b2': _L0_rec_in['b2'], 'L0_rec_w3': _L0_rec_in['w3'], 'L0_rec_b3': _L0_rec_in['b3']}

def reference(r_queries, r_user_behaviors, r_masks, L0_rec_w1, L0_rec_b1, L0_rec_w2, L0_rec_b2, L0_rec_w3, L0_rec_b3):
    import jax
    import jax.numpy as jnp

    def _L0_rec_ref(queries, user_behaviors, masks, w1, b1, w2, b2, w3, b3):
        import jax, jax.numpy as jnp
        import numpy as np
        NEG_LARGE = -2.0 ** 32 + 1.0
        B, L, twoD = user_behaviors.shape
        q = jnp.broadcast_to(queries[:, None, :], (B, L, twoD))
        feats = jnp.concatenate([q, user_behaviors, q - user_behaviors, q * user_behaviors], axis=-1)
        h = jax.nn.sigmoid(jnp.einsum('blf,fh->blh', feats, w1) + b1)
        h = jax.nn.sigmoid(jnp.einsum('blh,hk->blk', h, w2) + b2)
        scores = jnp.einsum('blk,ko->blo', h, w3) + b3
        valid = (masks != 0)[:, :, None]
        scores = jnp.where(valid, scores, NEG_LARGE)
        attn = jax.nn.softmax(scores, axis=1)
        return jnp.sum(attn * user_behaviors, axis=1)
    y = _L0_rec_ref(r_queries, r_user_behaviors, r_masks, L0_rec_w1, L0_rec_b1, L0_rec_w2, L0_rec_b2, L0_rec_w3, L0_rec_b3)
    return y

_drawn_inputs = setup_inputs


def setup_inputs(seed=0):
    import zlib

    import numpy as np

    out = dict(_drawn_inputs(seed))
    spreads = {'L0_rec_b1': (0.0, 0.8), 'L0_rec_b2': (0.0, 0.8)}
    factors = {'r_queries': 7.184, 'L0_rec_w1': 3.929, 'L0_rec_w2': 3.992, 'L0_rec_w3': 4.194}
    for name, (base, spread) in spreads.items():
        noise = np.random.default_rng([zlib.crc32(name.encode()), seed]).standard_normal(out[name].shape)
        drawn = base * np.exp(spread * noise) if base else spread * noise
        out[name] = jnp.asarray(drawn.astype(out[name].dtype))
    for name, factor in factors.items():
        out[name] = (out[name] * factor).astype(out[name].dtype)
    return out
```

```python
import concourse.bass as bass
from concourse import mybir
from contextlib import ExitStack

USERS, L, D = 2048, 200, 128
H1, H2 = 80, 40
G = 16
S = 128 // G
R = L // S
GROUPS = USERS // G
UNROLL = 4
TURNS = GROUPS // UNROLL
DEPTH = 3
GC = G * L
NEG_LARGE = -2.0 ** 32

TB = 4
T_CHUNKS = [(a, min(a + TB, R)) for a in range(0, R, TB)]
NT = len(T_CHUNKS)
PAIRS = G // 2
QUARTERS = 4
QU = G // QUARTERS
L2_CHUNKS = [(0, 9), (9, 17), (17, 25)]
N2 = len(L2_CHUNKS)
COLT = 4

C_IDENT, C_BLOCK, C_SEL, C_AUG2, C_AUG3, C_END = 0, 128, 144, 160, 160 + 81, 160 + 81 + 41


def pooling_program(nc, x, qT, masks, w1, b1, w2, b2, w3, b3, consts, out):
    fp32, bf16, fp16 = mybir.dt.float32, mybir.dt.bfloat16, mybir.dt.float16
    ALU, ACT, AX = mybir.AluOpType, mybir.ActivationFunctionType, mybir.AxisListType

    x_v = x.rearrange("(g u) (s r) d -> g (u s) (r d)", u=G, s=S)
    out_v = out.rearrange("(g u) d -> g u d", u=G)

    def reached(g, n):
        return not isinstance(g, int) or g >= n

    def live(g):
        return not isinstance(g, int) or 0 <= g < GROUPS

    def periods(eng, period):
        for k in range(UNROLL):
            period(k, k)
        with eng.Fori(1, TURNS) as i:
            for k in range(UNROLL):
                period(i * UNROLL + k, k)
        for k in range(DEPTH):
            period(GROUPS + k, k)

    with ExitStack() as ctx:
        def sb(name, shape, dt=fp32):
            return ctx.enter_context(nc.sbuf_tensor(name, shape, dt))

        def sem(name):
            return ctx.enter_context(nc.semaphore(name))

        con = sb("con", [128, C_END])
        ident = con[:, C_IDENT:C_IDENT + 128]
        block16 = con[:, C_BLOCK:C_BLOCK + G]
        sel = con[:, C_SEL:C_SEL + G]
        aug2 = con[0:H1 + 1, C_AUG2:C_AUG2 + H1 + 1]
        aug3 = con[0:H2 + 1, C_AUG3:C_AUG3 + H2 + 1]
        q_all = sb("q_all", [128, USERS])
        w1_sb = sb("w1_sb", [128, 4, H1])
        w_qac = sb("w_qac", [128, H1])
        w_xbc = sb("w_xbc", [128, H1])
        b1_sb = sb("b1_sb", [H1, 1])
        w2_in = sb("w2_in", [H1 + 1, H2])
        w2_f = sb("w2_f", [H1 + 1, 2, H2])
        w2_parts = sb("w2_parts", [H1 + 1, 3, H2], bf16)
        w3_in = sb("w3_in", [H2 + 1, 1])
        w3_wide = sb("w3_wide", [H2 + 1, 128])
        w3_b = sb("w3_b", [128, H2 + 1])
        bias_all = sb("bias_all", [H1, USERS])
        valid_i = sb("valid_i", [128, GROUPS * R], mybir.dt.int32)
        valid_all = valid_i[:, :].bitcast(fp32)
        minus_one = sb("minus_one", [1, 1])

        xs = sb("xs", [128, UNROLL, R, D])
        xT = sb("xT", [128, 2, G, R, S])
        wb = sb("wb", [128, 2, G, H1])
        bias = sb("bias", [H1, 2, G])
        t1 = sb("t1", [H1, 2, R, G, S])
        t1_hi = sb("t1_hi", [128, 2, R, G, S], fp16)
        t1_lo = sb("t1_lo", [H1, 2, R, G, S], fp16)
        t2 = sb("t2", [128, 2, R, H2])
        prod = sb("prod", [128, R, H2])
        score = sb("score", [128, 4, R])
        pen = sb("pen", [128, R])
        pmax = sb("pmax", [128, 1])
        umax = sb("umax", [1, G])
        umax_wide = sb("umax_wide", [1, G, S])
        neg_max = sb("neg_max", [128, 1])
        e = sb("e", [128, R])
        e_sum = sb("e_sum", [128, 1])
        e_block = sb("e_block", [128, R, G])
        acc_sb = sb("acc_sb", [128, D])
        recip = sb("recip", [G, 1])
        out_sb = sb("out_sb", [G, UNROLL, D])

        bank = [ctx.enter_context(nc.psum_tensor(f"bank{i}", [128, 512], fp32)) for i in range(8)]
        xT_ps, z1_ps, z2_ps, acc_ps, misc_ps = bank[0:2], bank[2:4], bank[4:6], bank[6], bank[7]
        pmaxT_ps = misc_ps[0:1, 0:128]
        neg_max_ps = misc_ps[:, 128:129]
        den_ps = misc_ps[0:G, 132:133]
        sum_ps = misc_ps[0:G, 256:256 + D]

        in_con, in_q, in_w1, in_small, in_mask = (sem(n) for n in ("in_con", "in_q", "in_w1", "in_small", "in_mask"))
        filled = sem("filled")
        w1_mixed = sem("w1_mixed")
        bias_mm = sem("bias_mm")
        bias_set = sem("bias_set")
        w3_widened = sem("w3_widened")
        w23_mm = sem("w23_mm")
        w2_step = sem("w2_step")
        w2_ready = sem("w2_ready")
        w3_ready = sem("w3_ready")
        mask_ready = sem("mask_ready")
        x_in = [sem(f"x_in{k}") for k in range(UNROLL)]
        xT_mm = sem("xT_mm")
        xT_out_a = sem("xT_out_a")
        xT_out_v = sem("xT_out_v")
        wb_mul = sem("wb_mul")
        wb_ready = sem("wb_ready")
        bias_ready = sem("bias_ready")
        z1_mm = sem("z1_mm")
        t1_done = sem("t1_done")
        hi_done = sem("hi_done")
        lo_pool = sem("lo_pool")
        lo_dve = sem("lo_dve")
        z2_mm = sem("z2_mm")
        t2_done = sem("t2_done")
        prod_done = sem("prod_done")
        sum_done = sem("sum_done")
        pen_done = sem("pen_done")
        valid_done = sem("valid_done")
        score_done = sem("score_done")
        pmax_done = sem("pmax_done")
        pmaxT_mm = sem("pmaxT_mm")
        umax_done = sem("umax_done")
        umax_wide_done = sem("umax_wide_done")
        neg_max_mm = sem("neg_max_mm")
        neg_max_done = sem("neg_max_done")
        e_done = sem("e_done")
        e_block_done = sem("e_block_done")
        final_mm = sem("final_mm")
        acc_done = sem("acc_done")
        sum_mm = sem("sum_mm")
        recip_done = sem("recip_done")
        out_done = sem("out_done")
        stored = [sem(f"stored{k}") for k in range(UNROLL)]

        DVE_T = (1, 3, 5)
        ACT_T = tuple(j for j in range(NT) if j not in DVE_T)
        POOL_Q = (0, 1, 2)
        DVE_Q = (3,)
        NA, NV = len(ACT_T), len(DVE_T)

        def wait_xT_chunk(eng, g, j):
            if j in ACT_T:
                eng.wait_ge(xT_out_a, g * NA + ACT_T.index(j) + 1)
            else:
                eng.wait_ge(xT_out_v, g * NV + DVE_T.index(j) + 1)

        block = ctx.enter_context(nc.Block())

        @block.sync
        def _(sp):
            sp.dma_start(con[:, :], consts).then_inc(in_con, 16)
            sp.dma_start(w1_sb[:, :, :], w1.rearrange("(c p) h -> p c h", p=128)).then_inc(in_w1, 16)
            sp.dma_start(xs[:, 0, :, :].rearrange("p r d -> p (r d)"), x_v[0, :, :]).then_inc(x_in[0], 16)
            sp.dma_start(q_all[:, :], qT).then_inc(in_q, 16)
            sp.dma_start(b1_sb[:, :], b1.rearrange("(h a) -> h a", a=1)).then_inc(in_small, 16)
            sp.dma_start(w2_in[0:H1, :], w2).then_inc(in_small, 16)
            sp.dma_start(w2_in[H1:H1 + 1, :], b2.rearrange("(a h) -> a h", a=1)).then_inc(in_small, 16)
            sp.dma_start(w3_in[0:H2, :], w3).then_inc(in_small, 16)
            sp.dma_start(w3_in[H2:H2 + 1, :], b3.rearrange("(a h) -> a h", a=1)).then_inc(in_small, 16)
            for k in range(1, UNROLL):
                sp.dma_start(xs[:, k, :, :].rearrange("p r d -> p (r d)"), x_v[k, :, :]).then_inc(x_in[k], 16)
                if k == 1:
                    sp.dma_start(valid_i[:, :], masks).then_inc(in_mask, 16)
            with sp.Fori(1, TURNS) as i:
                for k in range(UNROLL):
                    g = i * UNROLL + k
                    sp.wait_ge(final_mm, g - UNROLL + 1)
                    sp.dma_start(xs[:, k, :, :].rearrange("p r d -> p (r d)"),
                                 x_v[bass.ds(g, 1), :, :].rearrange("a p n -> p (a n)")).then_inc(x_in[k], 16)
                    sp.wait_ge(out_done, g - UNROLL + 1)
                    sp.dma_start(out_v[bass.ds(g - UNROLL, 1), :, :].rearrange("a u d -> u (a d)"),
                                 out_sb[:, k, :]).then_inc(stored[k], 16)
            for k in range(UNROLL):
                sp.wait_ge(out_done, GROUPS - UNROLL + k + 1)
                sp.dma_start(out_v[GROUPS - UNROLL + k, :, :], out_sb[:, k, :]).then_inc(stored[k], 16)
            for k in range(UNROLL):
                sp.wait_ge(stored[k], 16 * TURNS)

        @block.gpsimd
        def _(pool):
            pool.wait_ge(in_w1, 16)
            pool.wait_ge(in_q, 16)
            pool.wait_ge(w1_mixed, 2)

            def period(p, k):
                if live(p):
                    if reached(p, 2):
                        pool.wait_ge(z1_mm, (p - 1) * PAIRS)
                    q_g = q_all[:, bass.ds(p * G, G)]
                    nc.gpsimd.tensor_tensor(wb[:, k % 2, :, :],
                                            w1_sb[:, 3, :].rearrange("p (a h) -> p a h", a=1).broadcast_to([128, G, H1]),
                                            q_g.rearrange("p (u a) -> p u a", a=1).broadcast_to([128, G, H1]),
                                            ALU.mult).then_inc(wb_mul, 1)
                    pool.wait_ge(wb_mul, p + 1)
                    nc.gpsimd.tensor_tensor(wb[:, k % 2, :, :], wb[:, k % 2, :, :],
                                            w_xbc[:, :].rearrange("p (a h) -> p a h", a=1).broadcast_to([128, G, H1]),
                                            ALU.add).then_inc(wb_ready, 1)
                    if reached(p, 2):
                        pool.wait_ge(t1_done, (p - 1) * PAIRS)
                    if isinstance(p, int) and p == 0:
                        pool.wait_ge(bias_set, USERS // 512)
                    nc.gpsimd.tensor_copy(bias[:, k % 2, :], bias_all[:, bass.ds(p * G, G)]).then_inc(bias_ready, 1)
                g, b = p - 1, (k - 1) % 2
                if live(g):
                    for n, m in enumerate(POOL_Q):
                        pool.wait_ge(hi_done, g * QUARTERS + m + 1)
                        if n == 0 and reached(g, 2):
                            pool.wait_ge(z2_mm, (g - 1) * N2)
                        us = slice(m * QU, (m + 1) * QU)
                        nc.gpsimd.tensor_tensor(t1_lo[:, b, :, us, :], t1[:, b, :, us, :], t1_hi[0:H1, b, :, us, :],
                                                ALU.subtract).then_inc(lo_pool, 1)

            periods(pool, period)

        @block.scalar
        def _(act):
            def period(p, k):
                g1, k1 = p - 1, (k - 1) % UNROLL
                g2, k2 = p - 2, (k - 2) % UNROLL
                g3 = p - 3
                if live(g3):
                    act.wait_ge(neg_max_mm, g3 + 1)
                    nc.scalar.copy(neg_max[:, :], neg_max_ps).then_inc(neg_max_done, 1)
                    act.wait_ge(neg_max_done, g3 + 1)
                    act.wait_ge(score_done, g3 + 1)
                    if reached(g3, 1):
                        act.wait_ge(e_block_done, g3)
                        act.wait_ge(final_mm, g3)
                    nc.scalar.activation(e[:, :], score[:, 3, :], ACT.Exp, bias=neg_max[:, :],
                                         accum_out=e_sum[:, :]).then_inc(e_done, 1)
                for j in range(PAIRS):
                    if live(p) and j in ACT_T:
                        a, z = T_CHUNKS[j]
                        act.wait_ge(xT_mm, p * NT + j + 1)
                        if j == ACT_T[0] and reached(p, 2):
                            act.wait_ge(z1_mm, (p - 1) * PAIRS)
                        nc.scalar.copy(xT[:, k % 2, :, a:z, :].rearrange("d u r s -> d r u s"),
                                       xT_ps[(NT * k + j) % 2][:, 0:(z - a) * 128]
                                       .rearrange("d (r u s) -> d r u s", u=G, s=S)).then_inc(xT_out_a, 1)
                    if live(g1):
                        act.wait_ge(z1_mm, g1 * PAIRS + j + 1)
                        if j == 0:
                            act.wait_ge(bias_ready, g1 + 1)
                            if reached(g1, 2):
                                act.wait_ge(lo_pool, (g1 - 1) * len(POOL_Q))
                                act.wait_ge(lo_dve, (g1 - 1) * len(DVE_Q))
                        for n in range(2):
                            u = 2 * j + n
                            last = nc.scalar.activation(
                                t1[:, k1 % 2, :, u, :],
                                z1_ps[j % 2][0:H1, n * L:(n + 1) * L].rearrange("h (r s) -> h r s", s=S),
                                ACT.Tanh, bias=bias[:, k1 % 2, u:u + 1], scale=0.5)
                        last.then_inc(t1_done, 1)
                    if live(g2) and 2 <= j < 2 + N2:
                        a, z = L2_CHUNKS[j - 2]
                        act.wait_ge(z2_mm, g2 * N2 + j - 2 + 1)
                        if j == 2 and reached(g2, 2):
                            act.wait_ge(prod_done, g2 - 1)
                        nc.scalar.activation(t2[:, k2 % 2, a:z, :].rearrange("p r h -> p (r h)"),
                                             z2_ps[(N2 * k2 + j - 2) % 2][:, 0:(z - a) * H2],
                                             ACT.Tanh, scale=0.5).then_inc(t2_done, 1)

            periods(act, period)

        @block.vector
        def _(dve):
            nc.vector.memset(t1_hi[64:96, :, :, :, :], 1.0).then_inc(filled, 1)
            nc.vector.memset(acc_ps[:, :], 0.0).then_inc(filled, 1)
            nc.vector.memset(minus_one[:, :], -1.0).then_inc(filled, 1)
            dve.wait_ge(in_w1, 16)
            nc.vector.tensor_tensor(w_qac[:, :], w1_sb[:, 0, :], w1_sb[:, 2, :], ALU.add).then_inc(w1_mixed, 1)
            nc.vector.tensor_tensor(w_xbc[:, :], w1_sb[:, 1, :], w1_sb[:, 2, :], ALU.subtract).then_inc(w1_mixed, 1)
            dve.wait_ge(in_small, 80)
            nc.vector.tensor_copy(w3_wide[:, :], w3_in[:, :].broadcast_to([H2 + 1, 128])).then_inc(w3_widened, 1)
            for n in range(USERS // 512):
                dve.wait_ge(bias_mm, n + 1)
                nc.vector.tensor_scalar(bias_all[:, n * 512:(n + 1) * 512], z1_ps[n % 2][0:H1, :],
                                        b1_sb[:, :], 0.5, ALU.add, ALU.mult).then_inc(bias_set, 1)
            dve.wait_ge(w23_mm, 2)
            nc.vector.tensor_copy(w3_b[:, :], z2_ps[1][:, 0:H2 + 1]).then_inc(w3_ready, 1)
            nc.vector.tensor_copy(w2_f[:, 0, :], z2_ps[0][0:H1 + 1, 0:H2]).then_inc(w2_step, 1)
            for n in range(3):
                dve.wait_ge(w2_step, 2 * n + 1)
                part = nc.vector.tensor_copy(w2_parts[:, n, :], w2_f[:, n % 2, :])
                if n == 2:
                    part.then_inc(w2_ready, 1)
                else:
                    part.then_inc(w2_step, 1)
                    dve.wait_ge(w2_step, 2 * n + 2)
                    nc.vector.tensor_tensor(w2_f[:, (n + 1) % 2, :], w2_f[:, n % 2, :], w2_parts[:, n, :],
                                            ALU.subtract).then_inc(w2_step, 1)
            dve.wait_ge(in_mask, 16)
            nc.vector.tensor_scalar(valid_all, valid_i[:, :], 0, None, ALU.not_equal).then_inc(mask_ready, 1)

            def period(p, k):
                g1, b1_ = p - 1, (k - 1) % 2
                g2, k2 = p - 2, (k - 2) % UNROLL
                g3, k3 = p - 3, (k - 3) % UNROLL
                for j in range(PAIRS):
                    if live(p) and j in DVE_T:
                        a, z = T_CHUNKS[j]
                        dve.wait_ge(xT_mm, p * NT + j + 1)
                        if j == DVE_T[0] and reached(p, 2):
                            dve.wait_ge(z1_mm, (p - 1) * PAIRS)
                        nc.vector.tensor_copy(xT[:, k % 2, :, a:z, :].rearrange("d u r s -> d r u s"),
                                              xT_ps[(NT * k + j) % 2][:, 0:(z - a) * 128]
                                              .rearrange("d (r u s) -> d r u s", u=G, s=S)).then_inc(xT_out_v, 1)
                    if live(g3) and j == 0:
                        dve.wait_ge(e_done, g3 + 1)
                        if reached(g3, 1):
                            dve.wait_ge(final_mm, g3)
                        nc.vector.tensor_tensor(
                            e_block[:, :, :],
                            e[:, :].rearrange("p (r a) -> p r a", a=1).broadcast_to([128, R, G]),
                            block16.rearrange("p (a u) -> p a u", a=1).broadcast_to([128, R, G]),
                            ALU.mult).then_inc(e_block_done, 1)
                    if live(g3) and j == 3:
                        dve.wait_ge(final_mm, g3 + 1)
                        if reached(g3, 1):
                            dve.wait_ge(sum_mm, g3)
                        nc.vector.tensor_copy(acc_sb[:, :], acc_ps[:, 0:D]).then_inc(acc_done, 1)
                    if live(g3) and j == 5:
                        dve.wait_ge(sum_mm, g3 + 1)
                        nc.vector.reciprocal(recip[:, :], den_ps).then_inc(recip_done, 1)
                        dve.wait_ge(recip_done, g3 + 1)
                        if reached(g3, UNROLL):
                            dve.wait_ge(stored[k3], (g3 - k3) * (16 // UNROLL))
                        nc.vector.tensor_scalar(out_sb[:, k3, :], sum_ps, recip[:, :], None,
                                                ALU.mult).then_inc(out_done, 1)
                    if live(g1) and j % 2 == 1:
                        m = j // 2
                        us = slice(m * QU, (m + 1) * QU)
                        dve.wait_ge(t1_done, g1 * PAIRS + j + 1)
                        if m == 0 and reached(g1, 2):
                            dve.wait_ge(z2_mm, (g1 - 1) * N2)
                        nc.vector.tensor_copy(t1_hi[0:H1, b1_, :, us, :], t1[:, b1_, :, us, :]).then_inc(hi_done, 1)
                        if m in DVE_Q:
                            dve.wait_ge(hi_done, g1 * QUARTERS + m + 1)
                            nc.vector.tensor_tensor(t1_lo[:, b1_, :, us, :], t1[:, b1_, :, us, :],
                                                    t1_hi[0:H1, b1_, :, us, :], ALU.subtract).then_inc(lo_dve, 1)
                    if live(g2) and j == 5:
                        dve.wait_ge(t2_done, (g2 + 1) * N2)
                        nc.vector.tensor_tensor(
                            prod[:, :, :], t2[:, k2 % 2, :, :],
                            w3_b[:, 0:H2].rearrange("p (a h) -> p a h", a=1).broadcast_to([128, R, H2]),
                            ALU.mult).then_inc(prod_done, 1)
                        valid_g = valid_all[:, bass.ds(g2 * R, R)]
                        nc.vector.tensor_scalar(pen[:, :], valid_g, -NEG_LARGE, NEG_LARGE,
                                                ALU.mult, ALU.add).then_inc(pen_done, 1)
                        dve.wait_ge(prod_done, g2 + 1)
                        nc.vector.tensor_reduce(score[:, 0, :], prod[:, :, :], AX.X, ALU.add).then_inc(sum_done, 1)
                        nc.vector.tensor_copy(score[:, 1, :], valid_g).then_inc(valid_done, 1)
                        dve.wait_ge(sum_done, g2 + 1)
                        dve.wait_ge(valid_done, 2 * g2 + 1)
                        nc.vector.scalar_tensor_tensor(score[:, 2, :], score[:, 0, :], w3_b[:, H2:H2 + 1],
                                                       score[:, 1, :], ALU.add, ALU.mult).then_inc(valid_done, 1)
                        dve.wait_ge(valid_done, 2 * g2 + 2)
                        dve.wait_ge(pen_done, g2 + 1)
                        if reached(g2, 1):
                            dve.wait_ge(e_done, g2)
                        nc.vector.tensor_tensor(score[:, 3, :], score[:, 2, :], pen[:, :],
                                                ALU.add).then_inc(score_done, 1)
                        dve.wait_ge(score_done, g2 + 1)
                        if reached(g2, 1):
                            dve.wait_ge(pmaxT_mm, g2)
                        nc.vector.tensor_reduce(pmax[:, :], score[:, 3, :], AX.X, ALU.max).then_inc(pmax_done, 1)
                if live(g2):
                    dve.wait_ge(pmaxT_mm, g2 + 1)
                    nc.vector.tensor_reduce(umax[:, :], pmaxT_ps.rearrange("a (u s) -> a u s", s=S),
                                            AX.X, ALU.max).then_inc(umax_done, 1)
                    dve.wait_ge(umax_done, g2 + 1)
                    if reached(g2, 1):
                        dve.wait_ge(neg_max_mm, g2)
                    nc.vector.tensor_copy(umax_wide[:, :, :],
                                          umax[:, :].rearrange("a (u b) -> a u b", b=1).broadcast_to([1, G, S])
                                          ).then_inc(umax_wide_done, 1)

            periods(dve, period)

        @block.tensor
        def _(pe):
            pe.wait_ge(in_con, 16)
            pe.wait_ge(filled, 3)
            pe.wait_ge(in_q, 16)
            pe.wait_ge(w1_mixed, 2)
            for n in range(USERS // 512):
                if n >= 2:
                    pe.wait_ge(bias_set, n - 1)
                nc.tensor.matmul(z1_ps[n % 2][0:H1, :], w_qac[:, :], q_all[:, n * 512:(n + 1) * 512],
                                 start=True, stop=True).then_inc(bias_mm, 1)
            pe.wait_ge(in_small, 80)
            nc.tensor.matmul(z2_ps[0][0:H1 + 1, 0:H2], aug2, w2_in[:, :], start=True, stop=True).then_inc(w23_mm, 1)
            pe.wait_ge(w3_widened, 1)
            nc.tensor.matmul(z2_ps[1][:, 0:H2 + 1], w3_wide[:, :], aug3, start=True, stop=True).then_inc(w23_mm, 1)
            pe.wait_ge(bias_set, USERS // 512)
            pe.wait_ge(w3_ready, 1)
            pe.wait_ge(w2_ready, 1)

            def period(p, k):
                g1, k1 = p - 1, (k - 1) % UNROLL
                g2, k2 = p - 2, (k - 2) % UNROLL
                g3, k3 = p - 3, (k - 3) % UNROLL
                for j in range(PAIRS):
                    if live(p) and j < NT:
                        a, z = T_CHUNKS[j]
                        if j == 0:
                            pe.wait_ge(x_in[k], (p - k) * (16 // UNROLL) + 16)
                        if j >= 2:
                            wait_xT_chunk(pe, p, j - 2)
                        elif reached(p, 1):
                            wait_xT_chunk(pe, p - 1, NT + j - 2)
                        for r in range(a, z):
                            last = nc.tensor.transpose(xT_ps[(NT * k + j) % 2][:, (r - a) * 128:(r - a + 1) * 128],
                                                       xs[:, k, r, :], ident)
                        last.then_inc(xT_mm, 1)
                    if live(g1):
                        if j == 0:
                            pe.wait_ge(wb_ready, g1 + 1)
                            pe.wait_ge(xT_out_a, (g1 + 1) * NA)
                            pe.wait_ge(xT_out_v, (g1 + 1) * NV)
                        if j >= 2:
                            pe.wait_ge(t1_done, g1 * PAIRS + j - 1)
                        elif reached(g1, 1):
                            pe.wait_ge(t1_done, g1 * PAIRS + j - 1)
                        for n in range(2):
                            u = 2 * j + n
                            last = nc.tensor.matmul(z1_ps[j % 2][0:H1, n * L:(n + 1) * L], wb[:, k1 % 2, u, :],
                                                    xT[:, k1 % 2, u, :, :].rearrange("d r s -> d (r s)"),
                                                    start=True, stop=True)
                        last.then_inc(z1_mm, 1)
                    if live(g2) and 2 <= j < 2 + N2:
                        c = j - 2
                        a, z = L2_CHUNKS[c]
                        if c == 0:
                            pe.wait_ge(lo_pool, (g2 + 1) * len(POOL_Q))
                            pe.wait_ge(lo_dve, (g2 + 1) * len(DVE_Q))
                        if c >= 2 or reached(g2, 1):
                            pe.wait_ge(t2_done, g2 * N2 + c - 1)
                        for r in range(a, z):
                            to = z2_ps[(N2 * k2 + c) % 2][:, (r - a) * H2:(r - a + 1) * H2]
                            hi = t1_hi[0:H1 + 1, k2 % 2, r, :, :].rearrange("h u s -> h (u s)")
                            lo = t1_lo[:, k2 % 2, r, :, :].rearrange("h u s -> h (u s)")
                            for n in range(3):
                                nc.tensor.matmul(to, hi, w2_parts[:, n, :], start=(n == 0), stop=False)
                            for n in range(2):
                                last = nc.tensor.matmul(to, lo, w2_parts[0:H1, n, :], start=False, stop=(n == 1))
                        last.then_inc(z2_mm, 1)
                    if live(g3) and j == 0:
                        pe.wait_ge(umax_wide_done, g3 + 1)
                        nc.tensor.matmul(neg_max_ps, umax_wide[:, :, :].rearrange("a u s -> a (u s)"),
                                         minus_one[:, :], start=True, stop=True).then_inc(neg_max_mm, 1)
                    if live(g3) and j == 2:
                        pe.wait_ge(e_block_done, g3 + 1)
                        nc.tensor.matmul(den_ps, block16, e_sum[:, :], start=True, stop=True)
                        for r in range(R):
                            c = r % COLT
                            last = nc.tensor.matmul(acc_ps[32 * c:32 * c + G, 0:D], e_block[:, r, :], xs[:, k3, r, :],
                                                    start=(r < COLT), stop=(r >= R - COLT))
                        last.then_inc(final_mm, 1)
                    if live(g3) and j == 4:
                        pe.wait_ge(acc_done, g3 + 1)
                        nc.tensor.matmul(sum_ps, sel, acc_sb[:, :], start=True, stop=True).then_inc(sum_mm, 1)
                    if live(g2) and j == PAIRS - 1:
                        pe.wait_ge(pmax_done, g2 + 1)
                        if reached(g2, 1):
                            pe.wait_ge(out_done, g2)
                        nc.tensor.transpose(pmaxT_ps, pmax[:, :], ident).then_inc(pmaxT_mm, 1)

            periods(pe, period)


_ORDER = ["r_user_behaviors", "qT", "masks", "L0_rec_w1", "L0_rec_b1", "L0_rec_w2", "L0_rec_b2",
          "L0_rec_w3", "L0_rec_b3", "consts"]


def kernel(**inputs):
    import numpy as np
    import concourse.bacc as bacc
    from concourse import mybir as m
    from concourse.bass_utils import run_bass_kernel_spmd

    consts = np.zeros((128, C_END), np.float32)
    consts[:, C_IDENT:C_IDENT + 128] = np.eye(128)
    for p in range(128):
        consts[p, C_BLOCK + p // S] = 1.0
        if p % 32 < G:
            consts[p, C_SEL + p % 32] = 1.0
    for at, n in ((C_AUG2, H1), (C_AUG3, H2)):
        for j in range(n):
            consts[j, at + j] = 0.5
            consts[j, at + n] = 0.5
        consts[n, at + n] = 1.0

    given = dict(inputs)
    given["qT"] = np.asarray(inputs["r_queries"]).T
    given["masks"] = np.asarray(inputs["r_masks"]).reshape(GROUPS, G * S, R).transpose(1, 0, 2).reshape(G * S, GROUPS * R)
    given["consts"] = consts

    nc = bacc.Bacc("TRN2", target_bir_lowering=False, num_devices=1)
    arrays, args = {}, []
    for name in _ORDER:
        a = np.ascontiguousarray(given[name])
        arrays[f"in_{name}"] = a
        args.append(nc.dram_tensor(f"in_{name}", a.shape, m.dt.from_np(a.dtype), kind="ExternalInput").ap())
    out = nc.dram_tensor("out_0", (USERS, D), m.dt.float32, kind="ExternalOutput").ap()
    pooling_program(nc, *args, out)
    r = run_bass_kernel_spmd(nc, [arrays], core_ids=[0])
    return r.results[0]["out_0"]
```

```python
import concourse.bass as bass
from concourse import mybir
from contextlib import ExitStack

USERS, L, D = 2048, 200, 128
H1, H2 = 80, 40
G = 16
S = 128 // G
R = L // S
GROUPS = USERS // G
UNROLL = 6
TURNS = GROUPS // UNROLL
DEPTH = 4
GC = G * L
NEG_LARGE = -2.0 ** 32

TB = 4
T_CHUNKS = [(a, min(a + TB, R)) for a in range(0, R, TB)]
NT = len(T_CHUNKS)
PAIRS = G // 2
QUARTERS = 4
QU = G // QUARTERS
L2_CHUNKS = [(0, 9), (9, 17), (17, 25)]
N2 = len(L2_CHUNKS)
COLT = 4
W2_TOP = 13

L2_STEPS = [(0, 0, 3, (2, 2)), (0, 3, 6, (2, 3)), (0, 6, 9, (2, 4)), (1, 9, 13, (2, 5)),
            (1, 13, 17, (2, 6)), (2, 17, 21, (2, 7)), (2, 21, 25, (3, 0))]
T2_AT = [(2, 4), (2, 6), (3, 0)]
L3_AT = [(2, 5), (2, 7), (3, 1)]
SCORE_AT = (3, 2)
PMAX_AT = (3, 5)
NEG_MAX_AT = (3, 6)
EXP_AT = (3, 7)
F_AT = (4, 0)
ACC_AT = (4, 1)
SUM_AT = (4, 2)
OUT_AT = (4, 3)

C_IDENT, C_BLOCK, C_SEL, C_AUG2, C_AUG3, C_END = 0, 128, 144, 160, 160 + 81, 160 + 81 + 41


def pooling_program(nc, x, qT, masks, w1, b1, w2, b2, w3, b3, consts, out):
    fp32, fp16, int32 = mybir.dt.float32, mybir.dt.float16, mybir.dt.int32
    ALU, ACT, AX = mybir.AluOpType, mybir.ActivationFunctionType, mybir.AxisListType

    x_v = x.rearrange("(g u) (s r) d -> g (u s) (r d)", u=G, s=S)
    out_v = out.rearrange("(g u) d -> g u d", u=G)

    def reached(g, n):
        return not isinstance(g, int) or g >= n

    def live(g):
        return not isinstance(g, int) or 0 <= g < GROUPS

    def due(p, at, j):
        return j == at[1] and live(p - at[0])

    def periods(eng, period):
        for k in range(UNROLL):
            period(k, k, 0)
        with eng.Fori(1, TURNS) as i:
            for k in range(UNROLL):
                period(i * UNROLL + k, k, i)
        for p in range(TURNS * UNROLL, GROUPS + DEPTH):
            period(p, p % UNROLL, p // UNROLL)

    def lagging(p, k, t, lag):
        return p - lag, (k - lag) % UNROLL, t - 1 if k < lag else t

    with ExitStack() as ctx:
        def sb(name, shape, dt=fp32):
            return ctx.enter_context(nc.sbuf_tensor(name, shape, dt))

        def sem(name):
            return ctx.enter_context(nc.semaphore(name))

        con = sb("con", [128, C_END])
        ident = con[:, C_IDENT:C_IDENT + 128]
        block16 = con[:, C_BLOCK:C_BLOCK + G]
        sel = con[:, C_SEL:C_SEL + G]
        aug2 = con[0:H1 + 1, C_AUG2:C_AUG2 + H1 + 1]
        aug3 = con[0:H2 + 1, C_AUG3:C_AUG3 + H2 + 1]
        q_all = sb("q_all", [128, USERS])
        w1_sb = sb("w1_sb", [128, 4, H1])
        w_qac = sb("w_qac", [128, H1])
        w_xbc = sb("w_xbc", [128, H1])
        b1_sb = sb("b1_sb", [H1, 1])
        w2_in = sb("w2_in", [H1 + 1, H2])
        w2_f = sb("w2_f", [H1 + 1, H2])
        w2_parts = sb("w2_parts", [H1 + 1, 2, H2], fp16)
        w2_top = sb("w2_top", [128, 4])
        w2_scale = sb("w2_scale", [128, 2])
        w3_in = sb("w3_in", [H2 + 1, 1])
        w3_wide = sb("w3_wide", [H2 + 1, 128])
        w3_b = sb("w3_b", [128, H2 + 1])
        bias_all = sb("bias_all", [H1, USERS])
        valid_i = sb("valid_i", [128, GROUPS * R], int32)
        valid_all = valid_i[:, :].bitcast(fp32)
        minus_one = sb("minus_one", [1, 1])
        one_row = sb("one_row", [1, 128])

        xs = sb("xs", [128, UNROLL, R, D])
        xT = sb("xT", [128, 2, G, R, S])
        wb = sb("wb", [128, 2, G, H1])
        bias = sb("bias", [H1, 2, G])
        t1 = sb("t1", [H1, R, G, S])
        t1_hi = sb("t1_hi", [128, 2, R, G, S], fp16)
        t1_lo = sb("t1_lo", [H1, 2, R, G, S], fp16)
        t2 = sb("t2", [128, 2, R, H2])
        prod = sb("prod", [128, 2, R, H2])
        score = sb("score", [128, 3, R])
        pen = sb("pen", [128, R])
        pmax = sb("pmax", [128, 1])
        umax = sb("umax", [1, G])
        umax_wide = sb("umax_wide", [1, G, S])
        neg_max = sb("neg_max", [128, 1])
        e = sb("e", [128, R])
        e_sum = sb("e_sum", [128, 1])
        e_block = sb("e_block", [128, R, G])
        acc_sb = sb("acc_sb", [128, D])
        recip = sb("recip", [G, 1])
        out_sb = sb("out_sb", [G, UNROLL, D])

        bank = [ctx.enter_context(nc.psum_tensor(f"bank{i}", [128, 512], fp32)) for i in range(8)]
        xT_ps, z1_ps, z2_ps, acc_ps, misc_ps = bank[0:2], bank[2:4], bank[4:6], bank[6], bank[7]
        pmaxT_ps = misc_ps[0:1, 0:128]
        neg_max_ps = misc_ps[:, 128:129]
        den_ps = misc_ps[0:G, 132:133]
        sum_ps = misc_ps[0:G, 256:256 + D]

        in_con, in_q, in_w1, in_small, in_mask = (sem(n) for n in ("in_con", "in_q", "in_w1", "in_small", "in_mask"))
        filled = sem("filled")
        w1_mixed = sem("w1_mixed")
        bias_mm = sem("bias_mm")
        bias_set = sem("bias_set")
        w3_widened = sem("w3_widened")
        w23_mm = sem("w23_mm")
        w2_row_top = sem("w2_row_top")
        w2_topT = sem("w2_topT")
        w2_top_one = sem("w2_top_one")
        w2_top_mm = sem("w2_top_mm")
        w2_step = sem("w2_step")
        w2_ready = sem("w2_ready")
        w3_ready = sem("w3_ready")
        mask_ready = sem("mask_ready")
        x_in = [sem(f"x_in{k}") for k in range(UNROLL)]
        xT_mm = sem("xT_mm")
        xT_out_a = sem("xT_out_a")
        xT_out_v = sem("xT_out_v")
        wb_mul = sem("wb_mul")
        wb_ready = sem("wb_ready")
        bias_ready = sem("bias_ready")
        z1_mm = sem("z1_mm")
        t1_done = sem("t1_done")
        hi_done = sem("hi_done")
        lo_pool = sem("lo_pool")
        lo_dve = sem("lo_dve")
        z2_mm = sem("z2_mm")
        t2_done = sem("t2_done")
        prod_done = sem("prod_done")
        sum_done = sem("sum_done")
        pen_done = sem("pen_done")
        valid_done = sem("valid_done")
        score_done = sem("score_done")
        pmax_done = sem("pmax_done")
        pmaxT_mm = sem("pmaxT_mm")
        umax_done = sem("umax_done")
        umax_wide_done = sem("umax_wide_done")
        neg_max_mm = sem("neg_max_mm")
        neg_max_done = sem("neg_max_done")
        e_done = sem("e_done")
        e_block_done = sem("e_block_done")
        final_mm = sem("final_mm")
        acc_done = sem("acc_done")
        sum_mm = sem("sum_mm")
        recip_done = sem("recip_done")
        out_done = sem("out_done")
        stored = [sem(f"stored{k}") for k in range(UNROLL)]

        DVE_T = (0, 2, 4)
        ACT_T = tuple(j for j in range(NT) if j not in DVE_T)
        POOL_Q = (0, 1, 2)
        DVE_Q = (3,)
        NA, NV = len(ACT_T), len(DVE_T)

        def wait_xT_chunk(eng, g, j):
            if j in ACT_T:
                eng.wait_ge(xT_out_a, g * NA + ACT_T.index(j) + 1)
            else:
                eng.wait_ge(xT_out_v, g * NV + DVE_T.index(j) + 1)

        def wait_lo(eng, g, m):
            if m in POOL_Q:
                eng.wait_ge(lo_pool, g * len(POOL_Q) + POOL_Q.index(m) + 1)
            else:
                eng.wait_ge(lo_dve, g * len(DVE_Q) + DVE_Q.index(m) + 1)

        block = ctx.enter_context(nc.Block())

        @block.sync
        def _(sp):
            sp.dma_start(con[:, :], consts).then_inc(in_con, 16)
            sp.dma_start(w1_sb[:, :, :], w1.rearrange("(c p) h -> p c h", p=128)).then_inc(in_w1, 16)
            sp.dma_start(xs[:, 0, :, :].rearrange("p r d -> p (r d)"), x_v[0, :, :]).then_inc(x_in[0], 16)
            sp.dma_start(q_all[:, :], qT).then_inc(in_q, 16)
            sp.dma_start(b1_sb[:, :], b1.rearrange("(h a) -> h a", a=1)).then_inc(in_small, 16)
            sp.dma_start(w2_in[0:H1, :], w2).then_inc(in_small, 16)
            sp.dma_start(w2_in[H1:H1 + 1, :], b2.rearrange("(a h) -> a h", a=1)).then_inc(in_small, 16)
            sp.dma_start(w3_in[0:H2, :], w3).then_inc(in_small, 16)
            sp.dma_start(w3_in[H2:H2 + 1, :], b3.rearrange("(a h) -> a h", a=1)).then_inc(in_small, 16)
            for k in range(UNROLL):
                if k >= 1:
                    sp.dma_start(xs[:, k, :, :].rearrange("p r d -> p (r d)"), x_v[k, :, :]).then_inc(x_in[k], 16)
                if k == 1:
                    sp.dma_start(valid_i[:, :], masks).then_inc(in_mask, 16)
                sp.sem_inc(stored[k], 16)

            def load(g, k):
                sp.wait_ge(final_mm, g - UNROLL + 1)
                sp.dma_start(xs[:, k, :, :].rearrange("p r d -> p (r d)"),
                             x_v[bass.ds(g, 1), :, :].rearrange("a p n -> p (a n)")).then_inc(x_in[k], 16)

            def store(g, k):
                sp.wait_ge(out_done, g + 1)
                sp.dma_start(out_v[bass.ds(g, 1), :, :].rearrange("a u d -> u (a d)"),
                             out_sb[:, k, :]).then_inc(stored[k], 16)

            with sp.Fori(1, TURNS) as i:
                for k in range(UNROLL):
                    load(i * UNROLL + k, k)
                    store(i * UNROLL + k - UNROLL, k)
            for g in range(TURNS * UNROLL, GROUPS):
                load(g, g % UNROLL)
                store(g - UNROLL, g % UNROLL)
            for g in range(GROUPS - UNROLL, GROUPS):
                store(g, g % UNROLL)
            for k in range(UNROLL):
                sp.wait_ge(stored[k], 16 * (1 + len(range(k, GROUPS, UNROLL))))

        @block.gpsimd
        def _(pool):
            pool.wait_ge(in_w1, 16)
            pool.wait_ge(in_q, 16)
            pool.wait_ge(w1_mixed, 2)

            def period(p, k, t):
                if live(p):
                    if reached(p, 2):
                        pool.wait_ge(z1_mm, (p - 1) * PAIRS)
                    q_g = q_all[:, bass.ds(p * G, G)]
                    nc.gpsimd.tensor_tensor(wb[:, k % 2, :, :],
                                            w1_sb[:, 3, :].rearrange("p (a h) -> p a h", a=1).broadcast_to([128, G, H1]),
                                            q_g.rearrange("p (u a) -> p u a", a=1).broadcast_to([128, G, H1]),
                                            ALU.mult).then_inc(wb_mul, 1)
                    pool.wait_ge(wb_mul, p + 1)
                    nc.gpsimd.tensor_tensor(wb[:, k % 2, :, :], wb[:, k % 2, :, :],
                                            w_xbc[:, :].rearrange("p (a h) -> p a h", a=1).broadcast_to([128, G, H1]),
                                            ALU.add).then_inc(wb_ready, 1)
                    if reached(p, 2):
                        pool.wait_ge(t1_done, (p - 1) * PAIRS)
                    if isinstance(p, int) and p == 0:
                        pool.wait_ge(bias_set, USERS // 512)
                    nc.gpsimd.tensor_copy(bias[:, k % 2, :], bias_all[:, bass.ds(p * G, G)]).then_inc(bias_ready, 1)
                g, b = p - 1, (k - 1) % 2
                if live(g):
                    for n, m in enumerate(POOL_Q):
                        pool.wait_ge(hi_done, g * QUARTERS + m + 1)
                        if n == 0 and reached(g, 2):
                            pool.wait_ge(z2_mm, (g - 1) * N2)
                        us = slice(m * QU, (m + 1) * QU)
                        nc.gpsimd.tensor_tensor(t1_lo[:, b, :, us, :], t1[:, :, us, :], t1_hi[0:H1, b, :, us, :],
                                                ALU.subtract).then_inc(lo_pool, 1)

            periods(pool, period)

        @block.scalar
        def _(act):
            act.wait_ge(w2_step, 4)

            def period(p, k, t):
                g1 = p - 1
                g3 = p - 3
                for j in range(PAIRS):
                    if due(p, EXP_AT, j):
                        act.wait_ge(neg_max_mm, g3 + 1)
                        nc.scalar.copy(neg_max[:, :], neg_max_ps).then_inc(neg_max_done, 1)
                        act.wait_ge(neg_max_done, g3 + 1)
                        act.wait_ge(score_done, g3 + 1)
                        if reached(g3, 1):
                            act.wait_ge(e_block_done, g3)
                            act.wait_ge(final_mm, g3)
                        nc.scalar.activation(e[:, :], score[:, 2, :], ACT.Exp, bias=neg_max[:, :],
                                             accum_out=e_sum[:, :]).then_inc(e_done, 1)
                    if live(p) and j - 1 in ACT_T:
                        c = j - 1
                        a, z = T_CHUNKS[c]
                        act.wait_ge(xT_mm, p * NT + c + 1)
                        if c == ACT_T[0] and reached(p, 2):
                            act.wait_ge(z1_mm, (p - 1) * PAIRS)
                        nc.scalar.copy(xT[:, k % 2, :, a:z, :].rearrange("d u r s -> d r u s"),
                                       xT_ps[(NT * k + c) % 2][:, 0:(z - a) * 128]
                                       .rearrange("d (r u s) -> d r u s", u=G, s=S)).then_inc(xT_out_a, 1)
                    if live(g1):
                        act.wait_ge(z1_mm, g1 * PAIRS + j + 1)
                        if j == 0:
                            act.wait_ge(bias_ready, g1 + 1)
                        if j % 2 == 0 and reached(g1, 1):
                            wait_lo(act, g1 - 1, j // 2)
                        for n in range(2):
                            u = 2 * j + n
                            last = nc.scalar.activation(
                                t1[:, :, u, :],
                                z1_ps[j % 2][0:H1, n * L:(n + 1) * L].rearrange("h (r s) -> h r s", s=S),
                                ACT.Tanh, bias=bias[:, (k - 1) % 2, u:u + 1], scale=0.5)
                        last.then_inc(t1_done, 1)
                    for c, (a, z) in enumerate(L2_CHUNKS):
                        if due(p, T2_AT[c], j):
                            g, k2, _ = lagging(p, k, t, T2_AT[c][0])
                            act.wait_ge(z2_mm, g * N2 + c + 1)
                            if reached(g, 2):
                                act.wait_ge(prod_done, (g - 2) * N2 + c + 1)
                            nc.scalar.activation(t2[:, k2 % 2, a:z, :].rearrange("p r h -> p (r h)"),
                                                 z2_ps[(N2 * k2 + c) % 2][:, 0:(z - a) * H2],
                                                 ACT.Tanh, scale=w2_scale[:, 1:2]).then_inc(t2_done, 1)

            periods(act, period)

        @block.vector
        def _(dve):
            nc.vector.memset(t1_hi[64:96, :, :, :, :], 1.0).then_inc(filled, 1)
            nc.vector.memset(acc_ps[:, :], 0.0).then_inc(filled, 1)
            nc.vector.memset(minus_one[:, :], -1.0).then_inc(filled, 1)
            nc.vector.memset(one_row[:, :], 1.0).then_inc(filled, 1)
            nc.vector.memset(w2_top[:, :], 0.0).then_inc(filled, 1)
            dve.wait_ge(in_w1, 16)
            nc.vector.tensor_tensor(w_qac[:, :], w1_sb[:, 0, :], w1_sb[:, 2, :], ALU.add).then_inc(w1_mixed, 1)
            nc.vector.tensor_tensor(w_xbc[:, :], w1_sb[:, 1, :], w1_sb[:, 2, :], ALU.subtract).then_inc(w1_mixed, 1)
            dve.wait_ge(in_small, 80)
            nc.vector.tensor_copy(w3_wide[:, :], w3_in[:, :].broadcast_to([H2 + 1, 128])).then_inc(w3_widened, 1)
            for n in range(USERS // 512):
                dve.wait_ge(bias_mm, n + 1)
                nc.vector.tensor_scalar(bias_all[:, n * 512:(n + 1) * 512], z1_ps[n % 2][0:H1, :],
                                        b1_sb[:, :], 0.5, ALU.add, ALU.mult).then_inc(bias_set, 1)
            dve.wait_ge(w23_mm, 2)
            nc.vector.tensor_copy(w3_b[:, :], z2_ps[1][:, 0:H2 + 1]).then_inc(w3_ready, 1)
            w2_ps = z2_ps[0][0:H1 + 1, 0:H2]
            dve.wait_ge(filled, 5)
            nc.vector.tensor_reduce(w2_top[0:H1 + 1, 0:1], w2_ps, AX.X, ALU.max,
                                    apply_absolute_value=True).then_inc(w2_row_top, 1)
            dve.wait_ge(w2_topT, 1)
            nc.vector.tensor_reduce(w2_top[0:1, 1:2], misc_ps[0:1, 0:128], AX.X, ALU.max).then_inc(w2_top_one, 1)
            dve.wait_ge(w2_top_mm, 1)
            nc.vector.tensor_scalar(w2_top[:, 2:3], misc_ps[:, 128:129], 2.0 ** -90, None, ALU.max).then_inc(w2_step, 1)
            dve.wait_ge(w2_step, 1)
            top_bits, top_exp = w2_top[:, 2:3].bitcast(int32), w2_top[:, 3:4].bitcast(int32)
            nc.vector.tensor_scalar(top_exp, top_bits, 0x7F800000, None, ALU.bitwise_and).then_inc(w2_step, 1)
            dve.wait_ge(w2_step, 2)
            scale, inverse = w2_scale[:, 0:1].bitcast(int32), w2_scale[:, 1:2].bitcast(int32)
            nc.vector.tensor_scalar(scale, top_exp, -1.0, float((2 * 127 + W2_TOP) << 23),
                                    ALU.mult, ALU.add).then_inc(w2_step, 1)
            dve.wait_ge(w2_step, 3)
            nc.vector.tensor_scalar(inverse, scale, -1.0, float((2 * 127 - 1) << 23),
                                    ALU.mult, ALU.add).then_inc(w2_step, 1)
            nc.vector.tensor_scalar(w2_f[:, :], w2_ps, w2_scale[0:H1 + 1, 0:1], None, ALU.mult).then_inc(w2_step, 1)
            dve.wait_ge(w2_step, 5)
            nc.vector.tensor_copy(w2_parts[:, 0, :], w2_f[:, :]).then_inc(w2_step, 1)
            dve.wait_ge(w2_step, 6)
            nc.vector.tensor_tensor(w2_parts[:, 1, :], w2_f[:, :], w2_parts[:, 0, :], ALU.subtract).then_inc(w2_ready, 1)
            dve.wait_ge(in_mask, 16)
            nc.vector.tensor_scalar(valid_all, valid_i[:, :], 0, None, ALU.not_equal).then_inc(mask_ready, 1)

            def period(p, k, t):
                g1, b1_ = p - 1, (k - 1) % 2
                g3 = p - 3
                for j in range(PAIRS):
                    if due(p, PMAX_AT, j):
                        dve.wait_ge(pmaxT_mm, g3 + 1)
                        nc.vector.tensor_reduce(umax[:, :], pmaxT_ps.rearrange("a (u s) -> a u s", s=S),
                                                AX.X, ALU.max).then_inc(umax_done, 1)
                        dve.wait_ge(umax_done, g3 + 1)
                        if reached(g3, 1):
                            dve.wait_ge(neg_max_mm, g3)
                        nc.vector.tensor_copy(umax_wide[:, :, :],
                                              umax[:, :].rearrange("a (u b) -> a u b", b=1).broadcast_to([1, G, S])
                                              ).then_inc(umax_wide_done, 1)
                    if live(p) and j - 1 in DVE_T:
                        c = j - 1
                        a, z = T_CHUNKS[c]
                        dve.wait_ge(xT_mm, p * NT + c + 1)
                        if c == DVE_T[0] and reached(p, 2):
                            dve.wait_ge(z1_mm, (p - 1) * PAIRS)
                        nc.vector.tensor_copy(xT[:, k % 2, :, a:z, :].rearrange("d u r s -> d r u s"),
                                              xT_ps[(NT * k + c) % 2][:, 0:(z - a) * 128]
                                              .rearrange("d (r u s) -> d r u s", u=G, s=S)).then_inc(xT_out_v, 1)
                    if due(p, EXP_AT, j):
                        dve.wait_ge(e_done, g3 + 1)
                        if reached(g3, 1):
                            dve.wait_ge(final_mm, g3)
                        nc.vector.tensor_tensor(
                            e_block[:, :, :],
                            e[:, :].rearrange("p (r a) -> p r a", a=1).broadcast_to([128, R, G]),
                            block16.rearrange("p (a u) -> p a u", a=1).broadcast_to([128, R, G]),
                            ALU.mult).then_inc(e_block_done, 1)
                    if due(p, ACC_AT, j):
                        g = p - ACC_AT[0]
                        dve.wait_ge(final_mm, g + 1)
                        if reached(g, 1):
                            dve.wait_ge(sum_mm, g)
                        nc.vector.tensor_copy(acc_sb[:, :], acc_ps[:, 0:D]).then_inc(acc_done, 1)
                    if due(p, OUT_AT, j):
                        g, ko, used = lagging(p, k, t, OUT_AT[0])
                        dve.wait_ge(sum_mm, g + 1)
                        nc.vector.reciprocal(recip[:, :], den_ps).then_inc(recip_done, 1)
                        dve.wait_ge(recip_done, g + 1)
                        dve.wait_ge(stored[ko], used * 16 + 16)
                        nc.vector.tensor_scalar(out_sb[:, ko, :], sum_ps, recip[:, :], None,
                                                ALU.mult).then_inc(out_done, 1)
                    if live(g1) and j % 2 == 1:
                        m = j // 2
                        us = slice(m * QU, (m + 1) * QU)
                        dve.wait_ge(t1_done, g1 * PAIRS + j + 1)
                        if m == 0 and reached(g1, 2):
                            dve.wait_ge(z2_mm, (g1 - 1) * N2)
                        nc.vector.tensor_copy(t1_hi[0:H1, b1_, :, us, :], t1[:, :, us, :]).then_inc(hi_done, 1)
                        if m in DVE_Q:
                            dve.wait_ge(hi_done, g1 * QUARTERS + m + 1)
                            nc.vector.tensor_tensor(t1_lo[:, b1_, :, us, :], t1[:, :, us, :],
                                                    t1_hi[0:H1, b1_, :, us, :], ALU.subtract).then_inc(lo_dve, 1)
                    for c, (a, z) in enumerate(L2_CHUNKS):
                        if due(p, L3_AT[c], j):
                            g, k2, _ = lagging(p, k, t, L3_AT[c][0])
                            dve.wait_ge(t2_done, g * N2 + c + 1)
                            nc.vector.tensor_tensor(
                                prod[:, k2 % 2, a:z, :], t2[:, k2 % 2, a:z, :],
                                w3_b[:, 0:H2].rearrange("p (a h) -> p a h", a=1).broadcast_to([128, z - a, H2]),
                                ALU.mult).then_inc(prod_done, 1)
                            dve.wait_ge(prod_done, g * N2 + c + 1)
                            if c == 0 and reached(g, 1):
                                dve.wait_ge(valid_done, g)
                            nc.vector.tensor_reduce(score[:, 0, a:z], prod[:, k2 % 2, a:z, :], AX.X,
                                                    ALU.add).then_inc(sum_done, 1)
                    if due(p, SCORE_AT, j):
                        valid_g = valid_all[:, bass.ds(g3 * R, R)]
                        nc.vector.tensor_scalar(pen[:, :], valid_g, -NEG_LARGE, NEG_LARGE,
                                                ALU.mult, ALU.add).then_inc(pen_done, 1)
                        dve.wait_ge(sum_done, (g3 + 1) * N2)
                        nc.vector.scalar_tensor_tensor(score[:, 1, :], score[:, 0, :], w3_b[:, H2:H2 + 1],
                                                       valid_g, ALU.add, ALU.mult).then_inc(valid_done, 1)
                        dve.wait_ge(valid_done, g3 + 1)
                        dve.wait_ge(pen_done, g3 + 1)
                        if reached(g3, 1):
                            dve.wait_ge(e_done, g3)
                        nc.vector.tensor_tensor(score[:, 2, :], score[:, 1, :], pen[:, :],
                                                ALU.add).then_inc(score_done, 1)
                        dve.wait_ge(score_done, g3 + 1)
                        if reached(g3, 1):
                            dve.wait_ge(pmaxT_mm, g3)
                        nc.vector.tensor_reduce(pmax[:, :], score[:, 2, :], AX.X, ALU.max).then_inc(pmax_done, 1)

            periods(dve, period)

        @block.tensor
        def _(pe):
            pe.wait_ge(in_con, 16)
            pe.wait_ge(filled, 5)
            pe.wait_ge(in_q, 16)
            pe.wait_ge(w1_mixed, 2)
            for n in range(USERS // 512):
                if n >= 2:
                    pe.wait_ge(bias_set, n - 1)
                nc.tensor.matmul(z1_ps[n % 2][0:H1, :], w_qac[:, :], q_all[:, n * 512:(n + 1) * 512],
                                 start=True, stop=True).then_inc(bias_mm, 1)
            pe.wait_ge(in_small, 80)
            nc.tensor.matmul(z2_ps[0][0:H1 + 1, 0:H2], aug2, w2_in[:, :], start=True, stop=True).then_inc(w23_mm, 1)
            pe.wait_ge(w3_widened, 1)
            nc.tensor.matmul(z2_ps[1][:, 0:H2 + 1], w3_wide[:, :], aug3, start=True, stop=True).then_inc(w23_mm, 1)
            pe.wait_ge(w2_row_top, 1)
            nc.tensor.transpose(misc_ps[0:1, 0:128], w2_top[:, 0:1], ident).then_inc(w2_topT, 1)
            pe.wait_ge(w2_top_one, 1)
            nc.tensor.matmul(misc_ps[:, 128:129], one_row[:, :], w2_top[0:1, 1:2], start=True, stop=True).then_inc(w2_top_mm, 1)
            pe.wait_ge(bias_set, USERS // 512)
            pe.wait_ge(w3_ready, 1)
            pe.wait_ge(w2_ready, 1)

            def period(p, k, t):
                g1, k1, _ = lagging(p, k, t, 1)
                g3 = p - 3
                for j in range(PAIRS):
                    if due(p, PMAX_AT, j):
                        pe.wait_ge(pmax_done, g3 + 1)
                        if reached(g3, 1):
                            pe.wait_ge(out_done, g3)
                        nc.tensor.transpose(pmaxT_ps, pmax[:, :], ident).then_inc(pmaxT_mm, 1)
                    if due(p, NEG_MAX_AT, j):
                        pe.wait_ge(umax_wide_done, g3 + 1)
                        nc.tensor.matmul(neg_max_ps, umax_wide[:, :, :].rearrange("a u s -> a (u s)"),
                                         minus_one[:, :], start=True, stop=True).then_inc(neg_max_mm, 1)
                    if live(p) and j >= 1:
                        c = j - 1
                        a, z = T_CHUNKS[c]
                        if c == 0:
                            pe.wait_ge(x_in[k], t * 16 + 16)
                        if c >= 2:
                            wait_xT_chunk(pe, p, c - 2)
                        elif reached(p, 1):
                            wait_xT_chunk(pe, p - 1, NT + c - 2)
                        for r in range(a, z):
                            last = nc.tensor.transpose(xT_ps[(NT * k + c) % 2][:, (r - a) * 128:(r - a + 1) * 128],
                                                       xs[:, k, r, :], ident)
                        last.then_inc(xT_mm, 1)
                    if live(g1):
                        if j == 0:
                            pe.wait_ge(wb_ready, g1 + 1)
                            pe.wait_ge(xT_out_a, (g1 + 1) * NA)
                            pe.wait_ge(xT_out_v, (g1 + 1) * NV)
                        if j >= 2:
                            pe.wait_ge(t1_done, g1 * PAIRS + j - 1)
                        elif reached(g1, 1):
                            pe.wait_ge(t1_done, g1 * PAIRS + j - 1)
                        for n in range(2):
                            u = 2 * j + n
                            last = nc.tensor.matmul(z1_ps[j % 2][0:H1, n * L:(n + 1) * L], wb[:, k1 % 2, u, :],
                                                    xT[:, k1 % 2, u, :, :].rearrange("d r s -> d (r s)"),
                                                    start=True, stop=True)
                        last.then_inc(z1_mm, 1)
                    for c, a, z, at in L2_STEPS:
                        if due(p, at, j):
                            g, k2, _ = lagging(p, k, t, at[0])
                            first, end = L2_CHUNKS[c]
                            if a == 0:
                                pe.wait_ge(lo_pool, (g + 1) * len(POOL_Q))
                                pe.wait_ge(lo_dve, (g + 1) * len(DVE_Q))
                            if a == first and (c >= 2 or reached(g, 1)):
                                pe.wait_ge(t2_done, g * N2 + c - 1)
                            for r in range(a, z):
                                to = z2_ps[(N2 * k2 + c) % 2][:, (r - first) * H2:(r - first + 1) * H2]
                                hi = t1_hi[0:H1 + 1, k2 % 2, r, :, :].rearrange("h u s -> h (u s)")
                                lo = t1_lo[:, k2 % 2, r, :, :].rearrange("h u s -> h (u s)")
                                nc.tensor.matmul(to, hi, w2_parts[:, 0, :], start=True, stop=False)
                                nc.tensor.matmul(to, hi, w2_parts[:, 1, :], start=False, stop=False)
                                last = nc.tensor.matmul(to, lo, w2_parts[0:H1, 0, :], start=False, stop=True)
                            if z == end:
                                last.then_inc(z2_mm, 1)
                    if due(p, F_AT, j):
                        g, kf, _ = lagging(p, k, t, F_AT[0])
                        pe.wait_ge(e_block_done, g + 1)
                        nc.tensor.matmul(den_ps, block16, e_sum[:, :], start=True, stop=True)
                        for r in range(R):
                            c = r % COLT
                            last = nc.tensor.matmul(acc_ps[32 * c:32 * c + G, 0:D], e_block[:, r, :], xs[:, kf, r, :],
                                                    start=(r < COLT), stop=(r >= R - COLT))
                        last.then_inc(final_mm, 1)
                    if due(p, SUM_AT, j):
                        g = p - SUM_AT[0]
                        pe.wait_ge(acc_done, g + 1)
                        nc.tensor.matmul(sum_ps, sel, acc_sb[:, :], start=True, stop=True).then_inc(sum_mm, 1)

            periods(pe, period)


_ORDER = ["r_user_behaviors", "qT", "masks", "L0_rec_w1", "L0_rec_b1", "L0_rec_w2", "L0_rec_b2",
          "L0_rec_w3", "L0_rec_b3", "consts"]


def kernel(**inputs):
    import numpy as np
    import concourse.bacc as bacc
    from concourse import mybir as m
    from concourse.bass_utils import run_bass_kernel_spmd

    consts = np.zeros((128, C_END), np.float32)
    consts[:, C_IDENT:C_IDENT + 128] = np.eye(128)
    for p in range(128):
        consts[p, C_BLOCK + p // S] = 1.0
        if p % 32 < G:
            consts[p, C_SEL + p % 32] = 1.0
    for at, n in ((C_AUG2, H1), (C_AUG3, H2)):
        for j in range(n):
            consts[j, at + j] = 0.5
            consts[j, at + n] = 0.5
        consts[n, at + n] = 1.0

    given = dict(inputs)
    given["qT"] = np.asarray(inputs["r_queries"]).T
    given["masks"] = np.asarray(inputs["r_masks"]).reshape(GROUPS, G * S, R).transpose(1, 0, 2).reshape(G * S, GROUPS * R)
    given["consts"] = consts

    nc = bacc.Bacc("TRN2", target_bir_lowering=False, num_devices=1)
    arrays, args = {}, []
    for name in _ORDER:
        a = np.ascontiguousarray(given[name])
        arrays[f"in_{name}"] = a
        args.append(nc.dram_tensor(f"in_{name}", a.shape, m.dt.from_np(a.dtype), kind="ExternalInput").ap())
    out = nc.dram_tensor("out_0", (USERS, D), m.dt.float32, kind="ExternalOutput").ap()
    pooling_program(nc, *args, out)
    r = run_bass_kernel_spmd(nc, [arrays], core_ids=[0])
    return r.results[0]["out_0"]
```

```python
import concourse.bass as bass
from concourse import mybir
from contextlib import ExitStack

USERS, L, D = 2048, 200, 128
H1, H2 = 80, 40
G = 16
S = 128 // G
R = L // S
GROUPS = USERS // G
UNROLL = 6
TURNS = GROUPS // UNROLL
DEPTH = 5
GC = G * L
NEG_LARGE = -2.0 ** 32

TB = 4
T_CHUNKS = [(a, min(a + TB, R)) for a in range(0, R, TB)]
NT = len(T_CHUNKS)
PAIRS = G // 2
QUARTERS = 4
QU = G // QUARTERS
L2_CHUNKS = [(0, 9), (9, 17), (17, 25)]
N2 = len(L2_CHUNKS)
NXT, NZ1, NZ2 = 2, 2, 2
COLT = 4
W2_TOP = 13

L2_STEPS = [(0, 0, 3, (2, 3)), (0, 3, 6, (2, 4)), (0, 6, 9, (2, 5)), (1, 9, 13, (2, 6)),
            (1, 13, 17, (2, 7)), (2, 17, 21, (3, 0)), (2, 21, 25, (3, 1))]
T2_AT = [(2, 5), (2, 7), (3, 1)]
L3_AT = [(2, 7), (3, 1), (3, 1)]
SCORE_AT = (3, 4)
PMAX_AT = (3, 7)
UMAX_AT = (4, 1)
NEG_MAX_AT = (4, 3)
EXP_AT = (4, 3)
BLOCK_AT = (4, 6)
F_AT = (4, 7)
ACC_AT = (5, 1)
SUM_AT = (5, 3)
OUT_AT = (5, 7)

C_IDENT, C_BLOCK, C_SEL, C_AUG2, C_AUG3, C_END = 0, 128, 144, 160, 160 + 81, 160 + 81 + 41


def pooling_program(nc, x, qT, masks, w1, b1, w2, b2, w3, b3, consts, out):
    fp32, fp16, int32 = mybir.dt.float32, mybir.dt.float16, mybir.dt.int32
    ALU, ACT, AX = mybir.AluOpType, mybir.ActivationFunctionType, mybir.AxisListType

    x_v = x.rearrange("(g u) (s r) d -> g (u s) (r d)", u=G, s=S)
    out_v = out.rearrange("(g u) d -> g u d", u=G)

    def reached(g, n):
        return not isinstance(g, int) or g >= n

    def live(g):
        return not isinstance(g, int) or 0 <= g < GROUPS

    def due(p, at, j):
        return j == at[1] and live(p - at[0])

    def periods(eng, period):
        for k in range(UNROLL):
            period(k, k, 0)
        with eng.Fori(1, TURNS) as i:
            for k in range(UNROLL):
                period(i * UNROLL + k, k, i)
        for p in range(TURNS * UNROLL, GROUPS + DEPTH):
            period(p, p % UNROLL, p // UNROLL)

    def lagging(p, k, t, lag):
        return p - lag, (k - lag) % UNROLL, t - 1 if k < lag else t

    with ExitStack() as ctx:
        def sb(name, shape, dt=fp32):
            return ctx.enter_context(nc.sbuf_tensor(name, shape, dt))

        def sem(name):
            return ctx.enter_context(nc.semaphore(name))

        con = sb("con", [128, C_END])
        ident = con[:, C_IDENT:C_IDENT + 128]
        block16 = con[:, C_BLOCK:C_BLOCK + G]
        sel = con[:, C_SEL:C_SEL + G]
        aug2 = con[0:H1 + 1, C_AUG2:C_AUG2 + H1 + 1]
        aug3 = con[0:H2 + 1, C_AUG3:C_AUG3 + H2 + 1]
        q_all = sb("q_all", [128, USERS])
        w1_sb = sb("w1_sb", [128, 4, H1])
        w_qac = sb("w_qac", [128, H1])
        w_xbc = sb("w_xbc", [128, H1])
        b1_sb = sb("b1_sb", [H1, 1])
        w2_in = sb("w2_in", [H1 + 1, H2])
        w2_f = sb("w2_f", [H1 + 1, H2])
        w2_parts = sb("w2_parts", [H1 + 1, 2, H2], fp16)
        w2_top = sb("w2_top", [128, 4])
        w2_scale = sb("w2_scale", [128, 2])
        w3_in = sb("w3_in", [H2 + 1, 1])
        w3_wide = sb("w3_wide", [H2 + 1, 128])
        w3_b = sb("w3_b", [128, H2 + 1])
        bias_all = sb("bias_all", [H1, USERS])
        valid_i = sb("valid_i", [128, GROUPS * R], int32)
        valid_all = valid_i[:, :].bitcast(fp32)
        minus_one = sb("minus_one", [1, 1])
        one_row = sb("one_row", [1, 128])

        xs = sb("xs", [128, UNROLL, R, D])
        xT = sb("xT", [128, 2, G, R, S])
        wb = sb("wb", [128, 2, G, H1])
        bias = sb("bias", [H1, 2, G])
        t1 = sb("t1", [H1, R, G, S])
        t1_hi = sb("t1_hi", [128, 2, R, G, S], fp16)
        t1_lo = sb("t1_lo", [H1, 2, R, G, S], fp16)
        t2 = sb("t2", [128, 2, R, H2])
        prod = sb("prod", [128, 2, R, H2])
        score = sb("score", [128, 3, R])
        pen = sb("pen", [128, R])
        pmax = sb("pmax", [128, 1])
        umax = sb("umax", [1, G])
        umax_wide = sb("umax_wide", [1, G, S])
        neg_max = sb("neg_max", [128, 1])
        e = sb("e", [128, R])
        e_sum = sb("e_sum", [128, 1])
        e_block = sb("e_block", [128, R, G])
        acc_sb = sb("acc_sb", [128, D])
        recip = sb("recip", [G, 1])
        out_sb = sb("out_sb", [G, UNROLL, D])

        bank = [ctx.enter_context(nc.psum_tensor(f"bank{i}", [128, 512], fp32)) for i in range(8)]
        xT_ps, z1_ps, z2_ps = bank[0:NXT], bank[NXT:NXT + NZ1], bank[NXT + NZ1:NXT + NZ1 + NZ2]
        acc_ps, max_ps = bank[NXT + NZ1 + NZ2], bank[7]
        pmaxT_ps = max_ps[0:1, 0:128]
        neg_max_ps = max_ps[:, 128:129]
        den_ps = acc_ps[0:G, 132:133]
        sum_ps = acc_ps[0:G, 256:256 + D]

        in_con, in_q, in_w1, in_small, in_mask = (sem(n) for n in ("in_con", "in_q", "in_w1", "in_small", "in_mask"))
        filled = sem("filled")
        w1_mixed = sem("w1_mixed")
        bias_mm = sem("bias_mm")
        bias_set = sem("bias_set")
        w3_widened = sem("w3_widened")
        w23_mm = sem("w23_mm")
        w2_row_top = sem("w2_row_top")
        w2_topT = sem("w2_topT")
        w2_top_one = sem("w2_top_one")
        w2_top_mm = sem("w2_top_mm")
        w2_step = sem("w2_step")
        w2_ready = sem("w2_ready")
        w3_ready = sem("w3_ready")
        mask_ready = sem("mask_ready")
        x_in = [sem(f"x_in{k}") for k in range(UNROLL)]
        xT_mm = sem("xT_mm")
        xT_out_a = sem("xT_out_a")
        xT_out_v = sem("xT_out_v")
        wb_mul = sem("wb_mul")
        wb_ready = sem("wb_ready")
        bias_ready = sem("bias_ready")
        z1_mm = sem("z1_mm")
        t1_done = sem("t1_done")
        hi_done = sem("hi_done")
        lo_pool = sem("lo_pool")
        lo_dve = sem("lo_dve")
        z2_mm = sem("z2_mm")
        t2_done = sem("t2_done")
        prod_done = sem("prod_done")
        sum_done = sem("sum_done")
        pen_done = sem("pen_done")
        valid_done = sem("valid_done")
        score_done = sem("score_done")
        pmax_done = sem("pmax_done")
        pmaxT_mm = sem("pmaxT_mm")
        umax_done = sem("umax_done")
        umax_wide_done = sem("umax_wide_done")
        neg_max_mm = sem("neg_max_mm")
        neg_max_done = sem("neg_max_done")
        e_done = sem("e_done")
        e_block_done = sem("e_block_done")
        final_mm = sem("final_mm")
        acc_done = sem("acc_done")
        sum_mm = sem("sum_mm")
        recip_done = sem("recip_done")
        out_done = sem("out_done")
        stored = [sem(f"stored{k}") for k in range(UNROLL)]

        DVE_T = (0, 6)
        ACT_T = tuple(j for j in range(NT) if j not in DVE_T)
        POOL_Q = (1, 2, 3)
        DVE_Q = (0,)
        NA, NV = len(ACT_T), len(DVE_T)

        def wait_xT_chunk(eng, g, j):
            if j in ACT_T:
                eng.wait_ge(xT_out_a, g * NA + ACT_T.index(j) + 1)
            else:
                eng.wait_ge(xT_out_v, g * NV + DVE_T.index(j) + 1)

        def wait_lo(eng, g, m):
            if m in POOL_Q:
                eng.wait_ge(lo_pool, g * len(POOL_Q) + POOL_Q.index(m) + 1)
            else:
                eng.wait_ge(lo_dve, g * len(DVE_Q) + DVE_Q.index(m) + 1)

        block = ctx.enter_context(nc.Block())

        @block.sync
        def _(sp):
            sp.dma_start(con[:, :], consts).then_inc(in_con, 16)
            sp.dma_start(w1_sb[:, :, :], w1.rearrange("(c p) h -> p c h", p=128)).then_inc(in_w1, 16)
            sp.dma_start(xs[:, 0, :, :].rearrange("p r d -> p (r d)"), x_v[0, :, :]).then_inc(x_in[0], 16)
            sp.dma_start(q_all[:, :], qT).then_inc(in_q, 16)
            sp.dma_start(b1_sb[:, :], b1.rearrange("(h a) -> h a", a=1)).then_inc(in_small, 16)
            sp.dma_start(w2_in[0:H1, :], w2).then_inc(in_small, 16)
            sp.dma_start(w2_in[H1:H1 + 1, :], b2.rearrange("(a h) -> a h", a=1)).then_inc(in_small, 16)
            sp.dma_start(w3_in[0:H2, :], w3).then_inc(in_small, 16)
            sp.dma_start(w3_in[H2:H2 + 1, :], b3.rearrange("(a h) -> a h", a=1)).then_inc(in_small, 16)
            for k in range(UNROLL):
                if k >= 1:
                    sp.dma_start(xs[:, k, :, :].rearrange("p r d -> p (r d)"), x_v[k, :, :]).then_inc(x_in[k], 16)
                if k == 1:
                    sp.dma_start(valid_i[:, :], masks).then_inc(in_mask, 16)
                sp.sem_inc(stored[k], 16)

            def load(g, k):
                sp.wait_ge(final_mm, g - UNROLL + 1)
                sp.dma_start(xs[:, k, :, :].rearrange("p r d -> p (r d)"),
                             x_v[bass.ds(g, 1), :, :].rearrange("a p n -> p (a n)")).then_inc(x_in[k], 16)

            def store(g, k):
                sp.wait_ge(out_done, g + 1)
                sp.dma_start(out_v[bass.ds(g, 1), :, :].rearrange("a u d -> u (a d)"),
                             out_sb[:, k, :]).then_inc(stored[k], 16)

            with sp.Fori(1, TURNS) as i:
                for k in range(UNROLL):
                    load(i * UNROLL + k, k)
                    store(i * UNROLL + k - UNROLL, k)
            for g in range(TURNS * UNROLL, GROUPS):
                load(g, g % UNROLL)
                store(g - UNROLL, g % UNROLL)
            for g in range(GROUPS - UNROLL, GROUPS):
                store(g, g % UNROLL)
            for k in range(UNROLL):
                sp.wait_ge(stored[k], 16 * (1 + len(range(k, GROUPS, UNROLL))))

        @block.gpsimd
        def _(pool):
            pool.wait_ge(in_w1, 16)
            pool.wait_ge(in_q, 16)
            pool.wait_ge(w1_mixed, 2)

            def period(p, k, t):
                if live(p):
                    if reached(p, 2):
                        pool.wait_ge(z1_mm, (p - 1) * PAIRS)
                    q_g = q_all[:, bass.ds(p * G, G)]
                    nc.gpsimd.tensor_tensor(wb[:, k % 2, :, :],
                                            w1_sb[:, 3, :].rearrange("p (a h) -> p a h", a=1).broadcast_to([128, G, H1]),
                                            q_g.rearrange("p (u a) -> p u a", a=1).broadcast_to([128, G, H1]),
                                            ALU.mult).then_inc(wb_mul, 1)
                    pool.wait_ge(wb_mul, p + 1)
                    nc.gpsimd.tensor_tensor(wb[:, k % 2, :, :], wb[:, k % 2, :, :],
                                            w_xbc[:, :].rearrange("p (a h) -> p a h", a=1).broadcast_to([128, G, H1]),
                                            ALU.add).then_inc(wb_ready, 1)
                    if reached(p, 2):
                        pool.wait_ge(t1_done, (p - 1) * PAIRS)
                    if isinstance(p, int) and p == 0:
                        pool.wait_ge(bias_set, USERS // 512)
                    nc.gpsimd.tensor_copy(bias[:, k % 2, :], bias_all[:, bass.ds(p * G, G)]).then_inc(bias_ready, 1)
                g, b = p - 1, (k - 1) % 2
                if live(g):
                    for n, m in enumerate(POOL_Q):
                        pool.wait_ge(hi_done, g * QUARTERS + m + 1)
                        if n == 0 and reached(g, 2):
                            pool.wait_ge(z2_mm, (g - 1) * N2)
                        us = slice(m * QU, (m + 1) * QU)
                        nc.gpsimd.tensor_tensor(t1_lo[:, b, :, us, :], t1[:, :, us, :], t1_hi[0:H1, b, :, us, :],
                                                ALU.subtract).then_inc(lo_pool, 1)

            periods(pool, period)

        @block.scalar
        def _(act):
            act.wait_ge(w2_step, 4)

            def period(p, k, t):
                g1 = p - 1
                for j in range(PAIRS):
                    if live(p) and j - 1 in ACT_T:
                        c = j - 1
                        a, z = T_CHUNKS[c]
                        act.wait_ge(xT_mm, p * NT + c + 1)
                        if c == ACT_T[0] and reached(p, 2):
                            act.wait_ge(z1_mm, (p - 1) * PAIRS)
                        nc.scalar.copy(xT[:, k % 2, :, a:z, :].rearrange("d u r s -> d r u s"),
                                       xT_ps[(NT * k + c) % NXT][:, 0:(z - a) * 128]
                                       .rearrange("d (r u s) -> d r u s", u=G, s=S)).then_inc(xT_out_a, 1)
                    if live(g1):
                        act.wait_ge(z1_mm, g1 * PAIRS + j + 1)
                        if j == 0:
                            act.wait_ge(bias_ready, g1 + 1)
                        if j % 2 == 0 and reached(g1, 1):
                            wait_lo(act, g1 - 1, j // 2)
                        for n in range(2):
                            u = 2 * j + n
                            last = nc.scalar.activation(
                                t1[:, :, u, :],
                                z1_ps[(PAIRS * ((k - 1) % UNROLL) + j) % NZ1][0:H1, n * L:(n + 1) * L].rearrange("h (r s) -> h r s", s=S),
                                ACT.Tanh, bias=bias[:, (k - 1) % 2, u:u + 1], scale=0.5)
                        last.then_inc(t1_done, 1)
                    for c, (a, z) in enumerate(L2_CHUNKS):
                        if due(p, T2_AT[c], j):
                            g, k2, _ = lagging(p, k, t, T2_AT[c][0])
                            act.wait_ge(z2_mm, g * N2 + c + 1)
                            if reached(g, 2):
                                act.wait_ge(prod_done, (g - 2) * N2 + c + 1)
                            nc.scalar.activation(t2[:, k2 % 2, a:z, :].rearrange("p r h -> p (r h)"),
                                                 z2_ps[(N2 * k2 + c) % NZ2][:, 0:(z - a) * H2],
                                                 ACT.Tanh, scale=w2_scale[:, 1:2]).then_inc(t2_done, 1)
                    if due(p, EXP_AT, j):
                        g = p - EXP_AT[0]
                        act.wait_ge(neg_max_mm, g + 1)
                        nc.scalar.copy(neg_max[:, :], neg_max_ps).then_inc(neg_max_done, 1)
                        act.wait_ge(neg_max_done, g + 1)
                        act.wait_ge(score_done, g + 1)
                        if reached(g, 1):
                            act.wait_ge(e_block_done, g)
                            act.wait_ge(final_mm, g)
                        nc.scalar.activation(e[:, :], score[:, 2, :], ACT.Exp, bias=neg_max[:, :],
                                             accum_out=e_sum[:, :]).then_inc(e_done, 1)

            periods(act, period)

        @block.vector
        def _(dve):
            nc.vector.memset(t1_hi[64:96, :, :, :, :], 1.0).then_inc(filled, 1)
            nc.vector.memset(acc_ps[:, :], 0.0).then_inc(filled, 1)
            nc.vector.memset(minus_one[:, :], -1.0).then_inc(filled, 1)
            nc.vector.memset(one_row[:, :], 1.0).then_inc(filled, 1)
            nc.vector.memset(w2_top[:, :], 0.0).then_inc(filled, 1)
            dve.wait_ge(in_w1, 16)
            nc.vector.tensor_tensor(w_qac[:, :], w1_sb[:, 0, :], w1_sb[:, 2, :], ALU.add).then_inc(w1_mixed, 1)
            nc.vector.tensor_tensor(w_xbc[:, :], w1_sb[:, 1, :], w1_sb[:, 2, :], ALU.subtract).then_inc(w1_mixed, 1)
            dve.wait_ge(in_small, 80)
            nc.vector.tensor_copy(w3_wide[:, :], w3_in[:, :].broadcast_to([H2 + 1, 128])).then_inc(w3_widened, 1)
            for n in range(USERS // 512):
                dve.wait_ge(bias_mm, n + 1)
                nc.vector.tensor_scalar(bias_all[:, n * 512:(n + 1) * 512], z1_ps[n % 2][0:H1, :],
                                        b1_sb[:, :], 0.5, ALU.add, ALU.mult).then_inc(bias_set, 1)
            dve.wait_ge(w23_mm, 2)
            nc.vector.tensor_copy(w3_b[:, :], z2_ps[1][:, 0:H2 + 1]).then_inc(w3_ready, 1)
            w2_ps = z2_ps[0][0:H1 + 1, 0:H2]
            dve.wait_ge(filled, 5)
            nc.vector.tensor_reduce(w2_top[0:H1 + 1, 0:1], w2_ps, AX.X, ALU.max,
                                    apply_absolute_value=True).then_inc(w2_row_top, 1)
            dve.wait_ge(w2_topT, 1)
            nc.vector.tensor_reduce(w2_top[0:1, 1:2], max_ps[0:1, 0:128], AX.X, ALU.max).then_inc(w2_top_one, 1)
            dve.wait_ge(w2_top_mm, 1)
            nc.vector.tensor_scalar(w2_top[:, 2:3], max_ps[:, 128:129], 2.0 ** -90, None, ALU.max).then_inc(w2_step, 1)
            dve.wait_ge(w2_step, 1)
            top_bits, top_exp = w2_top[:, 2:3].bitcast(int32), w2_top[:, 3:4].bitcast(int32)
            nc.vector.tensor_scalar(top_exp, top_bits, 0x7F800000, None, ALU.bitwise_and).then_inc(w2_step, 1)
            dve.wait_ge(w2_step, 2)
            scale, inverse = w2_scale[:, 0:1].bitcast(int32), w2_scale[:, 1:2].bitcast(int32)
            nc.vector.tensor_scalar(scale, top_exp, -1.0, float((2 * 127 + W2_TOP) << 23),
                                    ALU.mult, ALU.add).then_inc(w2_step, 1)
            dve.wait_ge(w2_step, 3)
            nc.vector.tensor_scalar(inverse, scale, -1.0, float((2 * 127 - 1) << 23),
                                    ALU.mult, ALU.add).then_inc(w2_step, 1)
            nc.vector.tensor_scalar(w2_f[:, :], w2_ps, w2_scale[0:H1 + 1, 0:1], None, ALU.mult).then_inc(w2_step, 1)
            dve.wait_ge(w2_step, 5)
            nc.vector.tensor_copy(w2_parts[:, 0, :], w2_f[:, :]).then_inc(w2_step, 1)
            dve.wait_ge(w2_step, 6)
            nc.vector.tensor_tensor(w2_parts[:, 1, :], w2_f[:, :], w2_parts[:, 0, :], ALU.subtract).then_inc(w2_ready, 1)
            dve.wait_ge(in_mask, 16)
            nc.vector.tensor_scalar(valid_all, valid_i[:, :], 0, None, ALU.not_equal).then_inc(mask_ready, 1)

            def period(p, k, t):
                g1, b1_ = p - 1, (k - 1) % 2
                for j in range(PAIRS):
                    if due(p, UMAX_AT, j):
                        g = p - UMAX_AT[0]
                        dve.wait_ge(pmaxT_mm, g + 1)
                        nc.vector.tensor_reduce(umax[:, :], pmaxT_ps.rearrange("a (u s) -> a u s", s=S),
                                                AX.X, ALU.max).then_inc(umax_done, 1)
                        dve.wait_ge(umax_done, g + 1)
                        if reached(g, 1):
                            dve.wait_ge(neg_max_mm, g)
                        nc.vector.tensor_copy(umax_wide[:, :, :],
                                              umax[:, :].rearrange("a (u b) -> a u b", b=1).broadcast_to([1, G, S])
                                              ).then_inc(umax_wide_done, 1)
                    if due(p, BLOCK_AT, j):
                        g = p - BLOCK_AT[0]
                        dve.wait_ge(e_done, g + 1)
                        if reached(g, 1):
                            dve.wait_ge(final_mm, g)
                        nc.vector.tensor_tensor(
                            e_block[:, :, :],
                            e[:, :].rearrange("p (r a) -> p r a", a=1).broadcast_to([128, R, G]),
                            block16.rearrange("p (a u) -> p a u", a=1).broadcast_to([128, R, G]),
                            ALU.mult).then_inc(e_block_done, 1)
                    if due(p, ACC_AT, j):
                        g = p - ACC_AT[0]
                        dve.wait_ge(final_mm, g + 1)
                        if reached(g, 1):
                            dve.wait_ge(sum_mm, g)
                        nc.vector.tensor_copy(acc_sb[:, :], acc_ps[:, 0:D]).then_inc(acc_done, 1)
                    if due(p, OUT_AT, j):
                        g, ko, used = lagging(p, k, t, OUT_AT[0])
                        dve.wait_ge(sum_mm, g + 1)
                        nc.vector.reciprocal(recip[:, :], den_ps).then_inc(recip_done, 1)
                        dve.wait_ge(recip_done, g + 1)
                        dve.wait_ge(stored[ko], used * 16 + 16)
                        nc.vector.tensor_scalar(out_sb[:, ko, :], sum_ps, recip[:, :], None,
                                                ALU.mult).then_inc(out_done, 1)
                    if due(p, SCORE_AT, j):
                        g = p - SCORE_AT[0]
                        valid_g = valid_all[:, bass.ds(g * R, R)]
                        nc.vector.tensor_scalar(pen[:, :], valid_g, -NEG_LARGE, NEG_LARGE,
                                                ALU.mult, ALU.add).then_inc(pen_done, 1)
                        dve.wait_ge(sum_done, (g + 1) * N2)
                        nc.vector.scalar_tensor_tensor(score[:, 1, :], score[:, 0, :], w3_b[:, H2:H2 + 1],
                                                       valid_g, ALU.add, ALU.mult).then_inc(valid_done, 1)
                        dve.wait_ge(valid_done, g + 1)
                        dve.wait_ge(pen_done, g + 1)
                        if reached(g, 1):
                            dve.wait_ge(e_done, g)
                        nc.vector.tensor_tensor(score[:, 2, :], score[:, 1, :], pen[:, :],
                                                ALU.add).then_inc(score_done, 1)
                        dve.wait_ge(score_done, g + 1)
                        if reached(g, 1):
                            dve.wait_ge(pmaxT_mm, g)
                        nc.vector.tensor_reduce(pmax[:, :], score[:, 2, :], AX.X, ALU.max).then_inc(pmax_done, 1)
                    if live(p) and j - 1 in DVE_T:
                        c = j - 1
                        a, z = T_CHUNKS[c]
                        dve.wait_ge(xT_mm, p * NT + c + 1)
                        if c == DVE_T[0] and reached(p, 2):
                            dve.wait_ge(z1_mm, (p - 1) * PAIRS)
                        nc.vector.tensor_copy(xT[:, k % 2, :, a:z, :].rearrange("d u r s -> d r u s"),
                                              xT_ps[(NT * k + c) % NXT][:, 0:(z - a) * 128]
                                              .rearrange("d (r u s) -> d r u s", u=G, s=S)).then_inc(xT_out_v, 1)
                    if live(g1) and j % 2 == 1:
                        m = j // 2
                        us = slice(m * QU, (m + 1) * QU)
                        dve.wait_ge(t1_done, g1 * PAIRS + j + 1)
                        if m == 0 and reached(g1, 2):
                            dve.wait_ge(z2_mm, (g1 - 1) * N2)
                        nc.vector.tensor_copy(t1_hi[0:H1, b1_, :, us, :], t1[:, :, us, :]).then_inc(hi_done, 1)
                        if m in DVE_Q:
                            dve.wait_ge(hi_done, g1 * QUARTERS + m + 1)
                            nc.vector.tensor_tensor(t1_lo[:, b1_, :, us, :], t1[:, :, us, :],
                                                    t1_hi[0:H1, b1_, :, us, :], ALU.subtract).then_inc(lo_dve, 1)
                    for c, (a, z) in enumerate(L2_CHUNKS):
                        if due(p, L3_AT[c], j):
                            g, k2, _ = lagging(p, k, t, L3_AT[c][0])
                            dve.wait_ge(t2_done, g * N2 + c + 1)
                            nc.vector.tensor_tensor(
                                prod[:, k2 % 2, a:z, :], t2[:, k2 % 2, a:z, :],
                                w3_b[:, 0:H2].rearrange("p (a h) -> p a h", a=1).broadcast_to([128, z - a, H2]),
                                ALU.mult).then_inc(prod_done, 1)
                            dve.wait_ge(prod_done, g * N2 + c + 1)
                            if c == 0 and reached(g, 1):
                                dve.wait_ge(valid_done, g)
                            nc.vector.tensor_reduce(score[:, 0, a:z], prod[:, k2 % 2, a:z, :], AX.X,
                                                    ALU.add).then_inc(sum_done, 1)
            periods(dve, period)

        @block.tensor
        def _(pe):
            pe.wait_ge(in_con, 16)
            pe.wait_ge(filled, 5)
            pe.wait_ge(in_q, 16)
            pe.wait_ge(w1_mixed, 2)
            for n in range(USERS // 512):
                if n >= 2:
                    pe.wait_ge(bias_set, n - 1)
                nc.tensor.matmul(z1_ps[n % 2][0:H1, :], w_qac[:, :], q_all[:, n * 512:(n + 1) * 512],
                                 start=True, stop=True).then_inc(bias_mm, 1)
            pe.wait_ge(in_small, 80)
            nc.tensor.matmul(z2_ps[0][0:H1 + 1, 0:H2], aug2, w2_in[:, :], start=True, stop=True).then_inc(w23_mm, 1)
            pe.wait_ge(w3_widened, 1)
            nc.tensor.matmul(z2_ps[1][:, 0:H2 + 1], w3_wide[:, :], aug3, start=True, stop=True).then_inc(w23_mm, 1)
            pe.wait_ge(w2_row_top, 1)
            nc.tensor.transpose(max_ps[0:1, 0:128], w2_top[:, 0:1], ident).then_inc(w2_topT, 1)
            pe.wait_ge(w2_top_one, 1)
            nc.tensor.matmul(max_ps[:, 128:129], one_row[:, :], w2_top[0:1, 1:2], start=True, stop=True).then_inc(w2_top_mm, 1)
            pe.wait_ge(bias_set, USERS // 512)
            pe.wait_ge(w3_ready, 1)
            pe.wait_ge(w2_ready, 1)

            def period(p, k, t):
                g1, k1, _ = lagging(p, k, t, 1)
                for j in range(PAIRS):
                    if due(p, PMAX_AT, j):
                        g = p - PMAX_AT[0]
                        pe.wait_ge(pmax_done, g + 1)
                        if reached(g, 1):
                            pe.wait_ge(neg_max_done, g)
                        nc.tensor.transpose(pmaxT_ps, pmax[:, :], ident).then_inc(pmaxT_mm, 1)
                    if due(p, NEG_MAX_AT, j):
                        g = p - NEG_MAX_AT[0]
                        pe.wait_ge(umax_wide_done, g + 1)
                        nc.tensor.matmul(neg_max_ps, umax_wide[:, :, :].rearrange("a u s -> a (u s)"),
                                         minus_one[:, :], start=True, stop=True).then_inc(neg_max_mm, 1)
                    if live(p) and j >= 1:
                        c = j - 1
                        a, z = T_CHUNKS[c]
                        if c == 0:
                            pe.wait_ge(x_in[k], t * 16 + 16)
                        if c >= NXT:
                            wait_xT_chunk(pe, p, c - NXT)
                        elif reached(p, 1):
                            wait_xT_chunk(pe, p - 1, NT + c - NXT)
                        for r in range(a, z):
                            last = nc.tensor.transpose(xT_ps[(NT * k + c) % NXT][:, (r - a) * 128:(r - a + 1) * 128],
                                                       xs[:, k, r, :], ident)
                        last.then_inc(xT_mm, 1)
                    if live(g1):
                        if j == 0:
                            pe.wait_ge(wb_ready, g1 + 1)
                            pe.wait_ge(xT_out_a, (g1 + 1) * NA)
                            pe.wait_ge(xT_out_v, (g1 + 1) * NV)
                        if j >= NZ1 or reached(g1, 1):
                            pe.wait_ge(t1_done, g1 * PAIRS + j - NZ1 + 1)
                        for n in range(2):
                            u = 2 * j + n
                            last = nc.tensor.matmul(z1_ps[(PAIRS * ((k - 1) % UNROLL) + j) % NZ1][0:H1, n * L:(n + 1) * L], wb[:, k1 % 2, u, :],
                                                    xT[:, k1 % 2, u, :, :].rearrange("d r s -> d (r s)"),
                                                    start=True, stop=True)
                        last.then_inc(z1_mm, 1)
                    for c, a, z, at in L2_STEPS:
                        if due(p, at, j):
                            g, k2, _ = lagging(p, k, t, at[0])
                            first, end = L2_CHUNKS[c]
                            if a == 0:
                                pe.wait_ge(lo_pool, (g + 1) * len(POOL_Q))
                                pe.wait_ge(lo_dve, (g + 1) * len(DVE_Q))
                            if a == first and (c >= NZ2 or reached(g, 1)):
                                pe.wait_ge(t2_done, g * N2 + c - NZ2 + 1)
                            for r in range(a, z):
                                to = z2_ps[(N2 * k2 + c) % NZ2][:, (r - first) * H2:(r - first + 1) * H2]
                                hi = t1_hi[0:H1 + 1, k2 % 2, r, :, :].rearrange("h u s -> h (u s)")
                                lo = t1_lo[:, k2 % 2, r, :, :].rearrange("h u s -> h (u s)")
                                nc.tensor.matmul(to, hi, w2_parts[:, 0, :], start=True, stop=False)
                                nc.tensor.matmul(to, hi, w2_parts[:, 1, :], start=False, stop=False)
                                last = nc.tensor.matmul(to, lo, w2_parts[0:H1, 0, :], start=False, stop=True)
                            if z == end:
                                last.then_inc(z2_mm, 1)
                    if due(p, F_AT, j):
                        g, kf, _ = lagging(p, k, t, F_AT[0])
                        pe.wait_ge(e_block_done, g + 1)
                        if reached(g, 1):
                            pe.wait_ge(out_done, g)
                        nc.tensor.matmul(den_ps, block16, e_sum[:, :], start=True, stop=True)
                        for r in range(R):
                            c = r % COLT
                            last = nc.tensor.matmul(acc_ps[32 * c:32 * c + G, 0:D], e_block[:, r, :], xs[:, kf, r, :],
                                                    start=(r < COLT), stop=(r >= R - COLT))
                        last.then_inc(final_mm, 1)
                    if due(p, SUM_AT, j):
                        g = p - SUM_AT[0]
                        pe.wait_ge(acc_done, g + 1)
                        nc.tensor.matmul(sum_ps, sel, acc_sb[:, :], start=True, stop=True).then_inc(sum_mm, 1)

            periods(pe, period)


_ORDER = ["r_user_behaviors", "qT", "masks", "L0_rec_w1", "L0_rec_b1", "L0_rec_w2", "L0_rec_b2",
          "L0_rec_w3", "L0_rec_b3", "consts"]


def kernel(**inputs):
    import numpy as np
    import concourse.bacc as bacc
    from concourse import mybir as m
    from concourse.bass_utils import run_bass_kernel_spmd

    consts = np.zeros((128, C_END), np.float32)
    consts[:, C_IDENT:C_IDENT + 128] = np.eye(128)
    for p in range(128):
        consts[p, C_BLOCK + p // S] = 1.0
        if p % 32 < G:
            consts[p, C_SEL + p % 32] = 1.0
    for at, n in ((C_AUG2, H1), (C_AUG3, H2)):
        for j in range(n):
            consts[j, at + j] = 0.5
            consts[j, at + n] = 0.5
        consts[n, at + n] = 1.0

    given = dict(inputs)
    given["qT"] = np.asarray(inputs["r_queries"]).T
    given["masks"] = np.asarray(inputs["r_masks"]).reshape(GROUPS, G * S, R).transpose(1, 0, 2).reshape(G * S, GROUPS * R)
    given["consts"] = consts

    nc = bacc.Bacc("TRN2", target_bir_lowering=False, num_devices=1)
    arrays, args = {}, []
    for name in _ORDER:
        a = np.ascontiguousarray(given[name])
        arrays[f"in_{name}"] = a
        args.append(nc.dram_tensor(f"in_{name}", a.shape, m.dt.from_np(a.dtype), kind="ExternalInput").ap())
    out = nc.dram_tensor("out_0", (USERS, D), m.dt.float32, kind="ExternalOutput").ap()
    pooling_program(nc, *args, out)
    r = run_bass_kernel_spmd(nc, [arrays], core_ids=[0])
    return r.results[0]["out_0"]
```
